# Optimizing a Trainium2 kernel written in Bass

```python
import numpy as np
import jax
import jax.numpy as jnp

def _softmax(x, axis=-1):
    return jax.nn.softmax(x, axis=axis)

def _gelu(x):
    return jax.nn.gelu(x, approximate=True)

def _silu(x):
    return jax.nn.silu(x)

def _sigmoid(x):
    return jax.nn.sigmoid(x)

def _layernorm(x, axis=-1, eps=1e-05):
    m = jnp.mean(x, axis=axis, keepdims=True)
    v = jnp.var(x, axis=axis, keepdims=True)
    return (x - m) / jnp.sqrt(v + eps)

def _scatter_add(tgt, idx, src, axis=0):
    return tgt.at[idx].add(src)

def _segment_sum(src, seg, n):
    return jax.ops.segment_sum(src, seg, n)
kernel_name = 'mk_gnn_preln_d4_gnn_r32_70d7d1'

def setup_inputs(seed: int=0):
    np.random.seed(seed)
    _w = jnp.asarray

    def _rec_inputs():
        import jax
        import jax.numpy as jnp
        _gk = jax.random.key(seed)
        x = -0.0001006 + 1 * jax.random.normal(jax.random.fold_in(_gk, 1), (3125, 96), jnp.float32)
        src = jax.random.randint(jax.random.fold_in(_gk, 2), (100000,), 0, 3125, jnp.int32)
        dst = jnp.minimum((3125 * jax.random.uniform(jax.random.fold_in(_gk, 3), (100000,)) ** 2.0).astype(jnp.int32), 99999)
        _o = jnp.argsort(dst, stable=True)
        src = src[_o]
        dst = dst[_o]
        edge_attr_32 = 0.000196303 + 1.00016 * jax.random.normal(jax.random.fold_in(_gk, 12), (100000, 32), jnp.float32)
        edge_weight = 0.00107675 + 0.999702 * jax.random.normal(jax.random.fold_in(_gk, 14), (100000,), jnp.float32)
        return (x, src, dst, edge_attr_32, edge_weight)
    x, src, dst, edge_attr_32, edge_weight = _rec_inputs()

    def _L0_gnn_setup():
        import jax, jax.numpy as jnp
        import numpy as np
        N_NODES = 50000
        N_EDGES = 25000
        D = 96
        DEPTH = 2
        key = jax.random.key(seed)
        ks = jax.random.split(key, 8)
        scale = 1.0 / np.sqrt(D)
        x = jax.random.normal(ks[0], (N_NODES, D), dtype=jnp.float32)
        W0 = jax.random.normal(ks[1], (DEPTH, D, D), dtype=jnp.float32) * scale
        b0 = jnp.zeros((DEPTH, D), dtype=jnp.float32)
        W1 = jax.random.normal(ks[2], (DEPTH, D, D), dtype=jnp.float32) * scale
        b1 = jnp.zeros((DEPTH, D), dtype=jnp.float32)
        W2 = jax.random.normal(ks[3], (DEPTH, 2 * D, D), dtype=jnp.float32) * (1.0 / np.sqrt(2 * D))
        b2 = jnp.zeros((DEPTH, D), dtype=jnp.float32)
        edge_src = jax.random.randint(ks[4], (N_EDGES,), 0, N_NODES, dtype=jnp.int64 if jax.config.jax_enable_x64 else jnp.int32)
        edge_dst = jnp.sort(jax.random.randint(ks[5], (N_EDGES,), 0, N_NODES, dtype=jnp.int64 if jax.config.jax_enable_x64 else jnp.int32))
        return {'x': x, 'W0': W0, 'b0': b0, 'W1': W1, 'b1': b1, 'W2': W2, 'b2': b2, 'edge_src': edge_src, 'edge_dst': edge_dst}
    _L0_gnn_all = _L0_gnn_setup()
    _L0_gnn_in = {k: v for k, v in _L0_gnn_all.items() if k in ('W0', 'b0', 'W1', 'b1', 'W2', 'b2')}
    del _L0_gnn_all

    def _L1_gnn_setup():
        import jax, jax.numpy as jnp
        import numpy as np
        N_NODES = 50000
        N_EDGES = 25000
        D = 96
        key = jax.random.key(seed)
        k_x, k_pt, k_ei, k_ew, k_wv, k_bv = jax.random.split(key, 6)
        x = jax.random.normal(k_x, (N_NODES, D), dtype=jnp.float32)
        p_t = jax.random.normal(k_pt, (8, 16), dtype=jnp.float32)
        edge_index = jax.random.randint(k_ei, (2, N_EDGES), 0, N_NODES, dtype=jnp.int64)
        edge_weights = jax.random.normal(k_ew, (N_EDGES,), dtype=jnp.float32)
        lim = 1.0 / np.sqrt(D)
        Wv = jax.random.uniform(k_wv, (D, D), dtype=jnp.float32, minval=-lim, maxval=lim)
        bv = jax.random.uniform(k_bv, (D,), dtype=jnp.float32, minval=-lim, maxval=lim)
        return {'x': x, 'p_t': p_t, 'Wv': Wv, 'bv': bv, 'edge_weights': edge_weights, 'edge_index': edge_index}
    _L1_gnn_all = _L1_gnn_setup()
    _L1_gnn_in = {k: v for k, v in _L1_gnn_all.items() if k in ('p_t', 'Wv', 'bv')}
    del _L1_gnn_all

    def _L2_gnn_setup():
        import jax, jax.numpy as jnp
        import numpy as np
        N = 50000
        E = 25000
        D_IN = 96
        D_OUT = 96
        key = jax.random.key(seed)
        ks = jax.random.split(key, 6)
        x = jax.random.normal(ks[0], (N, D_IN), dtype=jnp.float32)
        edge_row = jax.random.randint(ks[1], (E,), 0, N, dtype=jnp.int32)
        edge_col = jax.random.randint(ks[2], (E,), 0, N, dtype=jnp.int32)
        edge_val = jax.random.uniform(ks[3], (E,), dtype=jnp.float32)
        bound = float(np.sqrt(6.0 / D_IN))
        weight = jax.random.uniform(ks[4], (D_IN, D_OUT), minval=-bound, maxval=bound, dtype=jnp.float32)
        b = jnp.zeros((D_OUT,), dtype=jnp.float32)
        return {'x': x, 'edge_row': edge_row, 'edge_col': edge_col, 'edge_val': edge_val, 'weight': weight, 'b': b}
    _L2_gnn_all = _L2_gnn_setup()
    _L2_gnn_in = {k: v for k, v in _L2_gnn_all.items() if k in ('weight', 'b')}
    del _L2_gnn_all

    def _L3_gnn_setup():
        import jax, jax.numpy as jnp
        import numpy as np
        N, E = (50000, 25000)
        ND, ED = (96, 32)

        def _gelu(x):
            return jax.nn.gelu(x, approximate=False)
        key = jax.random.key(seed)
        ks = jax.random.split(key, 16)
        s = lambda fan_in: 1.0 / np.sqrt(fan_in)
        inp = {'x': jax.random.normal(ks[0], (N, ND), jnp.float32), 'edge_index': jax.random.randint(ks[1], (2, E), 0, N, jnp.int32), 'edge_attr': jax.random.normal(ks[2], (E, ED), jnp.float32), 'mW1': jax.random.uniform(ks[3], (ND + ED, ND), jnp.float32, -s(ND + ED), s(ND + ED)), 'mb1': jnp.zeros((ND,), jnp.float32), 'mW2': jax.random.uniform(ks[4], (ND, ND), jnp.float32, -s(ND), s(ND)), 'mb2': jnp.zeros((ND,), jnp.float32), 'gW1': jax.random.uniform(ks[5], (ND + ED, ND), jnp.float32, -s(ND + ED), s(ND + ED)), 'gb1': jnp.zeros((ND,), jnp.float32), 'gW2': jax.random.uniform(ks[6], (ND, 1), jnp.float32, -s(ND), s(ND)), 'gb2': jnp.zeros((1,), jnp.float32), 'uW1': jax.random.uniform(ks[7], (2 * ND, ND), jnp.float32, -s(2 * ND), s(2 * ND)), 'ub1': jnp.zeros((ND,), jnp.float32), 'uW2': jax.random.uniform(ks[8], (ND, ND), jnp.float32, -s(ND), s(ND)), 'ub2': jnp.zeros((ND,), jnp.float32), 'ln_g': jnp.ones((ND,), jnp.float32), 'ln_b': jnp.zeros((ND,), jnp.float32)}
        return inp
    _L3_gnn_all = _L3_gnn_setup()
    _L3_gnn_in = {k: v for k, v in _L3_gnn_all.items() if k in ('mW1', 'mb1', 'mW2', 'mb2', 'gW1', 'gb1', 'gW2', 'gb2', 'uW1', 'ub1', 'uW2', 'ub2', 'ln_g', 'ln_b')}
    del _L3_gnn_all
    return {'x': x, 'src': src, 'dst': dst, 'edge_attr_32': edge_attr_32, 'edge_weight': edge_weight, 'L0_gnn_W0': _L0_gnn_in['W0'], 'L0_gnn_b0': _L0_gnn_in['b0'], 'L0_gnn_W1': _L0_gnn_in['W1'], 'L0_gnn_b1': _L0_gnn_in['b1'], 'L0_gnn_W2': _L0_gnn_in['W2'], 'L0_gnn_b2': _L0_gnn_in['b2'], 'L1_gnn_p_t': _L1_gnn_in['p_t'], 'L1_gnn_Wv': _L1_gnn_in['Wv'], 'L1_gnn_bv': _L1_gnn_in['bv'], 'L2_gnn_weight': _L2_gnn_in['weight'], 'L2_gnn_b': _L2_gnn_in['b'], 'L3_gnn_mW1': _L3_gnn_in['mW1'], 'L3_gnn_mb1': _L3_gnn_in['mb1'], 'L3_gnn_mW2': _L3_gnn_in['mW2'], 'L3_gnn_mb2': _L3_gnn_in['mb2'], 'L3_gnn_gW1': _L3_gnn_in['gW1'], 'L3_gnn_gb1': _L3_gnn_in['gb1'], 'L3_gnn_gW2': _L3_gnn_in['gW2'], 'L3_gnn_gb2': _L3_gnn_in['gb2'], 'L3_gnn_uW1': _L3_gnn_in['uW1'], 'L3_gnn_ub1': _L3_gnn_in['ub1'], 'L3_gnn_uW2': _L3_gnn_in['uW2'], 'L3_gnn_ub2': _L3_gnn_in['ub2'], 'L3_gnn_ln_g': _L3_gnn_in['ln_g'], 'L3_gnn_ln_b': _L3_gnn_in['ln_b']}

def reference(x, src, dst, edge_attr_32, edge_weight, L0_gnn_W0, L0_gnn_b0, L0_gnn_W1, L0_gnn_b1, L0_gnn_W2, L0_gnn_b2, L1_gnn_p_t, L1_gnn_Wv, L1_gnn_bv, L2_gnn_weight, L2_gnn_b, L3_gnn_mW1, L3_gnn_mb1, L3_gnn_mW2, L3_gnn_mb2, L3_gnn_gW1, L3_gnn_gb1, L3_gnn_gW2, L3_gnn_gb2, L3_gnn_uW1, L3_gnn_ub1, L3_gnn_uW2, L3_gnn_ub2, L3_gnn_ln_g, L3_gnn_ln_b):
    import jax
    import jax.numpy as jnp

    def _L0_gnn_ref(x, W0, b0, W1, b1, W2, b2, edge_src, edge_dst):
        import jax, jax.numpy as jnp
        import numpy as np
        N_NODES = 50000
        N_EDGES = 25000
        D = 96
        DEPTH = 2
        n = x.shape[0]
        depth = W0.shape[0]
        for i in range(depth):
            h_self = x @ W1[i] + b1[i]
            h_nb = x @ W0[i] + b0[i]
            agg = jax.ops.segment_sum(h_nb[edge_src], edge_dst, num_segments=n)
            x = jnp.concatenate([h_self, agg], axis=-1) @ W2[i] + b2[i]
            x = x / jnp.std(x, axis=-1, ddof=1, keepdims=True)
        return x

    def _L1_gnn_ref(x, p_t, Wv, bv, edge_weights, edge_index):
        import jax, jax.numpy as jnp
        import numpy as np
        N_NODES = 50000
        N_EDGES = 25000
        D = 96
        n = x.shape[0]
        tgt = edge_index[1]
        seg_max = jax.ops.segment_max(edge_weights, tgt, num_segments=n)
        e = jnp.exp(edge_weights - seg_max[tgt])
        denom = jax.ops.segment_sum(e, tgt, num_segments=n)
        gamma = e / denom[tgt]
        msg = jax.nn.relu(x[tgt] @ Wv + bv) * gamma[:, None]
        out = jax.ops.segment_sum(msg, tgt, num_segments=n)
        return out

    def _L2_gnn_ref(x, edge_row, edge_col, edge_val, weight, b):
        import jax, jax.numpy as jnp
        import numpy as np
        N = 50000
        E = 25000
        D_IN = 96
        D_OUT = 96
        support = x @ weight
        gathered = support[edge_col] * edge_val[:, None]
        out = jax.ops.segment_sum(gathered, edge_row, num_segments=x.shape[0])
        return out + b

    def _L3_gnn_ref(x, edge_index, edge_attr, mW1, mb1, mW2, mb2, gW1, gb1, gW2, gb2, uW1, ub1, uW2, ub2, ln_g, ln_b):
        import jax, jax.numpy as jnp
        import numpy as np
        N, E = (50000, 25000)
        ND, ED = (96, 32)

        def _gelu(x):
            return jax.nn.gelu(x, approximate=False)
        src, dst = (edge_index[0], edge_index[1])
        edge_input = jnp.concatenate([x[src], edge_attr], axis=-1)
        messages = _gelu(edge_input @ mW1 + mb1) @ mW2 + mb2
        gates = jax.nn.sigmoid(_gelu(edge_input @ gW1 + gb1) @ gW2 + gb2)
        aggregated = jax.ops.segment_sum(messages * gates, dst, num_segments=x.shape[0])
        combined = jnp.concatenate([x, aggregated], axis=-1)
        update = _gelu(combined @ uW1 + ub1) @ uW2 + ub2
        h = x + update
        mu = jnp.mean(h, axis=-1, keepdims=True)
        var = jnp.mean(jnp.square(h - mu), axis=-1, keepdims=True)
        return (h - mu) * jax.lax.rsqrt(var + 1e-05) * ln_g + ln_b
    edge_index = jnp.stack([src, dst])
    h = jnp.maximum(_layernorm(x, axis=-1), 0.0)
    x = x + _L0_gnn_ref(h, L0_gnn_W0, L0_gnn_b0, L0_gnn_W1, L0_gnn_b1, L0_gnn_W2, L0_gnn_b2, src, dst)
    h = jnp.maximum(_layernorm(x, axis=-1), 0.0)
    x = x + _L1_gnn_ref(h, L1_gnn_p_t, L1_gnn_Wv, L1_gnn_bv, edge_weight, edge_index)
    h = jnp.maximum(_layernorm(x, axis=-1), 0.0)
    x = x + _L2_gnn_ref(h, src, dst, edge_weight, L2_gnn_weight, L2_gnn_b)
    h = jnp.maximum(_layernorm(x, axis=-1), 0.0)
    x = x + _L3_gnn_ref(h, edge_index, edge_attr_32, L3_gnn_mW1, L3_gnn_mb1, L3_gnn_mW2, L3_gnn_mb2, L3_gnn_gW1, L3_gnn_gb1, L3_gnn_gW2, L3_gnn_gb2, L3_gnn_uW1, L3_gnn_ub1, L3_gnn_uW2, L3_gnn_ub2, L3_gnn_ln_g, L3_gnn_ln_b)
    return x

_drawn_inputs = setup_inputs


def setup_inputs(seed=0):
    import zlib

    import numpy as np

    out = dict(_drawn_inputs(seed))
    spreads = {'L0_gnn_b0': (0.0, 0.1),
     'L0_gnn_b1': (0.0, 0.8),
     'L0_gnn_b2': (0.0, 0.8),
     'L2_gnn_b': (0.0, 0.462),
     'L3_gnn_mb1': (0.0, 0.62),
     'L3_gnn_mb2': (0.0, 0.281),
     'L3_gnn_gb1': (0.0, 2.0),
     'L3_gnn_ub1': (0.0, 0.8),
     'L3_gnn_ub2': (0.0, 0.356),
     'L3_gnn_ln_g': (1.0, 0.2),
     'L3_gnn_ln_b': (0.0, 0.538)}
    factors = {'edge_attr_32': 6.591, 'L3_gnn_gW1': 8.0, 'L3_gnn_gW2': 8.0}
    for name, (base, spread) in spreads.items():
        noise = np.random.default_rng([zlib.crc32(name.encode()), seed]).standard_normal(out[name].shape)
        drawn = base * np.exp(spread * noise) if base else spread * noise
        out[name] = jnp.asarray(drawn.astype(out[name].dtype))
    for name, factor in factors.items():
        out[name] = (out[name] * factor).astype(out[name].dtype)
    return out
```

```python
from contextlib import ExitStack

import concourse.bass as bass
from concourse import mybir

ALU = mybir.AluOpType
ACT = mybir.ActivationFunctionType
AX_X = mybir.AxisListType.X
F32 = mybir.dt.float32
I32 = mybir.dt.int32

D = 96
DE = 32
NB = 25
BP = 125
N = NB * BP
EP, EC = 125, 800
E = EP * EC
T = 816
SETS, GT = 4, 4
BODY = SETS * GT
NI = T // BODY
NIS = EC // BODY
PW = 5 + DE
MW = D + 1
AW = D + 1
PER_BANK = 5
ROWS = 128 * T
BIG = 1e38
assert N == 3125 and E == 100000 and T * 128 >= E + 127 * NB and PER_BANK * AW <= 512

WEIGHTS = ["W0_0", "W0_1", "W1_0", "W1_1", "W2a_0", "W2a_1", "W2b_0", "W2b_1", "Wv", "Wl2",
           "mW1x", "gW1x", "mW1e", "gW1e", "mW2", "uW1a", "uW1b", "uW2"]
WEIGHT_LOADS = 35
WI = {n: i for i, n in enumerate(WEIGHTS)}

NODE_STEPS = [("h0T", 7), ("tab0", 5), ("self0", 7), ("agg0T", 7), ("z0", 5),
              ("h1T", 7), ("tab1", 5), ("self1", 7), ("agg1T", 7), ("z1", 5),
              ("h2T", 7), ("y", 5), ("h3T", 7), ("sup", 5),
              ("h4T", 7), ("tab3", 13), ("agg3T", 7), ("msgT", 7), ("uT", 7), ("up", 5)]
FIRST, SIZE = {}, {}
_n = 0
for _name, _k in NODE_STEPS:
    FIRST[_name], SIZE[_name] = _n, _k
    _n += _k


def following(i, k):
    return (i, k + 1) if k < SETS - 1 else (i + 1, 0)


def node_bank(g):
    return 5 + g % 3


def build(nc, a, out):
    ctx = ExitStack()
    with ctx:
        def sb(name, shape, dt=F32):
            return ctx.enter_context(nc.sbuf_tensor(name, shape, dt))

        def sem(name):
            return ctx.enter_context(nc.semaphore(name))

        payload = nc.dram_tensor("payload", (128, T * PW), F32, kind="Internal").ap()
        messages = nc.dram_tensor("messages", (128, T * MW), F32, kind="Internal").ap()
        payload_rows = payload.rearrange("p (t w) -> (p t) w", w=PW)
        message_rows = messages.rearrange("p (t w) -> (p t) w", w=MW)
        table = [nc.dram_tensor(f"table{d}", (N, D), F32, kind="Internal").ap() for d in range(2)]
        table3 = nc.dram_tensor("table3", (N, 2 * D), F32, kind="Internal").ap()

        x = sb("x", [BP, NB, D])
        h = sb("h", [BP, NB, D])
        z = sb("z", [BP, NB, D])
        tmp = sb("tmp", [BP, NB, D])
        agg = sb("agg", [BP, NB, AW])
        tab = sb("tab", [BP, NB * 2 * D])
        hT = sb("hT", [D + 1, N])
        wt = sb("wt", [D + 1, len(WEIGHTS), D])
        region = sb("region", [128, 11600])
        meta = region[0:EP, 0:EC * 5].rearrange("p (c w) -> p c w", w=5)

        def sort_array(i):
            return region[0:EP, (5 + i) * EC:(6 + i) * EC]

        key, blk, pos, mask, csum, prod, ones_row = (sort_array(i) for i in range(7))
        place = sort_array(7).bitcast(I32)
        tile_i = sort_array(8).bitcast(I32)
        row_i = csum.bitcast(I32)
        sT = region[0:D + 1, 0:N]
        aT = region[0:D + 1, N:2 * N]
        nmx_all = region[0:BP, 2 * N:2 * N + T]
        den_all = region[0:BP, 2 * N + T:2 * N + 2 * T]
        blk_t = sb("blk_t", [BP, T])
        seg_tmp = region[0:BP, 2 * N + 2 * T:2 * N + 3 * T]
        nmx_full = region[0:BP, 2 * N + 3 * T:2 * N + 4 * T]
        place_slot = sb("place_slot", [EP, SETS, GT], I32)
        acc_d = sb("acc_d", [1, T], I32)
        acc_s = sb("acc_s", [1, T], I32)
        sup_d = sb("sup_d", [1, T], I32)
        tile_row = region[0:1, 13 * EC:13 * EC + T]
        tile_step = region[0:1, 5 * EC:5 * EC + T]
        iota_i = sb("iota_i", [128, 128], I32)
        iota = sb("iota", [128, 128])
        part = sb("part", [128, 1])
        iota_t = sb("iota_t", [BP, T])
        ident = sb("ident", [128, 128])
        upper = sb("upper", [128, 128])
        ones = sb("ones", [128, 128])
        zrow = sb("zrow", [1, 512])
        count = sb("count", [EP, NB])
        base = sb("base", [EP, NB])
        need = sb("need", [EP, NB])
        need_i = sb("need_i", [EP, NB], I32)
        ends = sb("ends", [EP, NB])
        stat = sb("stat", [BP, 8, NB])
        seg_m = sb("seg_m", [BP, NB])
        seg_d = sb("seg_d", [BP, NB])
        share = sb("share", [BP, NB])
        l2b = sb("l2b", [BP, D])
        ln_g = sb("ln_g", [BP, D])
        ln_b = sb("ln_b", [BP, D])
        gw2 = sb("gw2", [128, D])
        gb2 = sb("gb2", [128, 1])
        pad_pay = sb("pad_pay", [128, 16, PW])
        edges = sb("edges", [128, SETS, GT, PW])
        index = sb("index", [128, SETS, GT], I32)
        gat = sb("gat", [128, SETS, GT, 2 * D])
        hot = sb("hot", [128, SETS, GT, BP])
        work = sb("work", [128, 4096])
        pen = work[:, 0:2000].rearrange("p (k j n) -> p k j n", k=SETS, j=GT)
        val = work[:, 2048:4048].rearrange("p (k j n) -> p k j n", k=SETS, j=GT)
        hotT = work[0:BP, 0:2048].rearrange("p (k e) -> p k e", k=SETS)
        pad_msg = work[:, 2048:2048 + 16 * MW].rearrange("p (t w) -> p t w", w=MW)
        msg = work[:, 2048:2048 + BODY * MW].rearrange("p (k j n) -> p k j n", k=SETS, j=GT)
        gel = work[:, 0:BODY * 2 * (D + 1)].rearrange("p (k j s n) -> p k j s n", k=SETS, j=GT, s=2)
        nmx = sb("nmx", [BP, SETS, GT])
        den = sb("den", [BP, SETS, GT])
        attrT = region[0:DE, 2 * N:2 * N + SETS * GT * 128].rearrange("p (k e) -> p k e", k=SETS)
        gprod = region[:, 8400:8400 + GT * D].rearrange("p (j f) -> p j f", j=GT)
        gsum = sb("gsum", [128, SETS, GT])
        gate = sb("gate", [128, SETS, GT])
        psum = ctx.enter_context(nc.psum_tensor("psum", [128, 8, 512], F32))
        acc = psum[0:BP, 0:5, :].rearrange("p a b -> p (a b)")

        s_w = sem("weights_loaded")
        s_x = sem("x_loaded")
        s_key = sem("keys_loaded")
        s_iota = sem("iotas_made")
        s_const = sem("constants_made")
        s_pad = sem("pad_tiles_made")
        s_padw = sem("payload_pads_written")
        s_padm = sem("message_pads_written")
        s_vl = sem("vector_link")
        s_al = sem("scalar_link")
        s_var = sem("variance_ready")
        s_sd = sem("sqrt_ready")
        s_h = sem("h_ready")
        s_mm = sem("node_group_done")
        s_ev = sem("node_group_evacuated")
        s_tab = sem("table_stored")
        s_cnt = sem("bucket_counts_ready")
        s_pre = sem("bucket_prefix_ready")
        s_meta = sem("meta_ready")
        s_agg = sem("agg_evacuated")
        s_norm = sem("node_update_done")
        s_seg = sem("segment_exponent_ready")
        s_segx = sem("segment_exp_done")
        s_out = sem("out_stored")
        s_res = sem("result_ready")

        def sems(name):
            return [sem(f"{name}{k}") for k in range(SETS)]

        s_fr = sems("slot_free")
        s_at = sems("attr_loaded")
        s_ms = sems("meta_in_slot")
        s_pl = sems("place_in_slot")
        s_sc = sems("payload_scattered")
        s_ed = sems("edges_loaded")
        s_ix = sems("index_ready")
        s_g = sems("rows_gathered")
        s_hot = sems("hot_ready")
        s_used = sems("group_used")
        s_pen = sems("penalty_ready")
        s_val = sems("masked_weights_ready")
        s_vt = sems("masked_weights_transposed")
        s_mx = sems("tile_max_ready")
        s_exp = sems("tile_exp_done")
        s_ht = sems("hot_transposed")
        s_hte = sems("hotT_evacuated")
        s_sup = sems("support_rows_ready")
        s_msg = sems("messages_ready")
        s_msc = sems("messages_scattered")
        s_attT = sems("attr_transposed")
        s_atte = sems("attrT_evacuated")
        s_pre3 = sems("edge_preactivation_ready")
        s_hid = sems("edge_hidden_ready")
        s_gel = sems("gelu_done")
        s_dot = sems("gate_dot_ready")
        s_gate = sems("tanh_ready")
        s_prod = sem("gate_products_ready")
        s_gst = sem("gate_steps")

        block = ctx.enter_context(nc.Block())

        @block.sync
        def _(sp):
            sp.dma_start(x[:, :, :], a["x"].rearrange("(b p) f -> p b f", p=BP)).then_inc(s_x, 16)
            sp.dma_start(key.bitcast(I32), a["dst"].rearrange("(p c) -> p c", p=EP)).then_inc(s_key, 16)
            sp.dma_start(csum.bitcast(I32), a["src"].rearrange("(p c) -> p c", p=EP)).then_inc(s_key, 16)
            sp.dma_start(prod, a["edge_weight"].rearrange("(p c) -> p c", p=EP)).then_inc(s_key, 16)

            def row(v):
                return v.rearrange("(o n) -> o n", o=1)

            def weight(name, w, b=None):
                sp.dma_start(wt[0:w.shape[0], WI[name], :], w).then_inc(s_w, 16)
                if b is not None:
                    sp.dma_start(wt[D:D + 1, WI[name], :], row(b)).then_inc(s_w, 16)

            for d in range(2):
                weight(f"W0_{d}", a["L0_gnn_W0"][d], a["L0_gnn_b0"][d])
                weight(f"W1_{d}", a["L0_gnn_W1"][d], a["L0_gnn_b1"][d])
                weight(f"W2a_{d}", a["L0_gnn_W2"][d, 0:D], a["L0_gnn_b2"][d])
                weight(f"W2b_{d}", a["L0_gnn_W2"][d, D:2 * D])
            weight("Wv", a["L1_gnn_Wv"], a["L1_gnn_bv"])
            weight("Wl2", a["L2_gnn_weight"])
            weight("mW1x", a["L3_gnn_mW1"][0:D], a["L3_gnn_mb1"])
            weight("gW1x", a["L3_gnn_gW1"][0:D], a["L3_gnn_gb1"])
            weight("mW1e", a["L3_gnn_mW1"][D:D + DE])
            weight("gW1e", a["L3_gnn_gW1"][D:D + DE])
            weight("mW2", a["L3_gnn_mW2"], a["L3_gnn_mb2"])
            weight("uW1a", a["L3_gnn_uW1"][0:D], a["L3_gnn_ub1"])
            weight("uW1b", a["L3_gnn_uW1"][D:2 * D])
            weight("uW2", a["L3_gnn_uW2"], a["L3_gnn_ub2"])
            for dst, v in ((l2b, "L2_gnn_b"), (ln_g, "L3_gnn_ln_g"), (ln_b, "L3_gnn_ln_b")):
                sp.dma_start(dst[:, :], a[v].partition_broadcast(BP)).then_inc(s_w, 16)
            sp.dma_start(gw2[:, :], a["L3_gnn_gW2"].rearrange("n o -> (n o)").partition_broadcast(128)).then_inc(s_w, 16)
            sp.dma_start(gb2[:, :], a["L3_gnn_gb2"].partition_broadcast(128)).then_inc(s_w, 16)

            sp.wait_ge(s_pad, 2)
            pad_pay_flat = pad_pay[:, :, :].rearrange("p t w -> p (t w)")
            pad_msg_flat = pad_msg[:, :, :].rearrange("p t w -> p (t w)")
            with sp.Fori(0, NI) as i:
                sp.dma_start(payload[:, bass.ds(i * 16 * PW, 16 * PW)], pad_pay_flat).then_inc(s_padw, 16)
            with sp.Fori(0, NI) as i:
                sp.dma_start(messages[:, bass.ds(i * 16 * MW, 16 * MW)], pad_msg_flat).then_inc(s_padm, 16)

            tab96 = tab[:, 0:NB * D].rearrange("p (b f) -> p b f", f=D)
            sp.wait_ge(s_ev, FIRST["tab0"] + SIZE["tab0"])
            sp.dma_start(table[0].rearrange("(b p) f -> p b f", p=BP), tab96).then_inc(s_tab, 16)

            attr = a["edge_attr_32"].rearrange("(p c) f -> p c f", p=EP)

            def load_attr(i, k):
                sp.sem_inc(s_fr[k], 1)
                sp.dma_start(edges[0:EP, k, :, 5:PW], attr[:, bass.ds(i * BODY + k * GT, GT), :]).then_inc(s_at[k], 16)

            for k in range(SETS):
                load_attr(0, k)
            with sp.Fori(1, NIS) as i:
                for k in range(SETS):
                    sp.wait_ge(s_sc[k], i * (16 * GT))
                    load_attr(i, k)
            for k in range(SETS):
                sp.wait_ge(s_sc[k], 16 * GT * NIS)

            def load_group(i, k):
                sp.dma_start(edges[:, k, :, :].rearrange("p j w -> p (j w)"),
                             payload[:, bass.ds((i * BODY + k * GT) * PW, GT * PW)]).then_inc(s_ed[k], 16)

            def load_edges(loop):
                with sp.Fori(0, NI) as i:
                    for k in range(SETS):
                        sp.wait_ge(s_used[k], i + (1 + loop * NI))
                        load_group(i, k)

            load_edges(0)
            sp.wait_ge(s_ev, FIRST["tab1"] + SIZE["tab1"])
            sp.dma_start(table[1].rearrange("(b p) f -> p b f", p=BP), tab96).then_inc(s_tab, 16)
            load_edges(1)
            for k in range(SETS):
                sp.wait_ge(s_used[k], 1 + 2 * NI)
                load_group(0, k)
            with sp.Fori(1, NI) as i:
                for k in range(SETS):
                    sp.wait_ge(s_msc[k], i * (16 * GT))
                    sp.sem_inc(s_used[k], 1)
                    load_group(i, k)
            for k in range(SETS):
                sp.wait_ge(s_msc[k], 16 * GT * NI)
                sp.sem_inc(s_used[k], 1)
            with sp.Fori(0, NI) as i:
                for k in range(SETS):
                    sp.wait_ge(s_used[k], i + (1 + 3 * NI))
                    sp.dma_start(msg[:, k, :, :].rearrange("p j w -> p (j w)"),
                                 messages[:, bass.ds((i * BODY + k * GT) * MW, GT * MW)]).then_inc(s_ed[k], 16)
            sp.wait_ge(s_ev, FIRST["tab3"] + SIZE["tab3"])
            sp.dma_start(table3.rearrange("(b p) f -> p b f", p=BP),
                         tab[:, :].rearrange("p (b f) -> p b f", f=2 * D)).then_inc(s_tab, 16)
            load_edges(4)
            sp.wait_ge(s_res, 1)
            sp.dma_start(out.rearrange("(b p) f -> p b f", p=BP), z[:, :, :]).then_inc(s_out, 16)
            sp.wait_ge(s_out, 16)

        @block.gpsimd
        def _(pool):
            pool.iota(iota_i[:, :], pattern=[[1, 128]], base=0, channel_multiplier=0).then_inc(s_iota, 1)
            pool.iota(part[:, :], pattern=[[0, 1]], base=0, channel_multiplier=1,
                      allow_small_or_imprecise_dtypes=True).then_inc(s_iota, 1)
            pool.iota(iota_t[:, :], pattern=[[1, T]], base=0, channel_multiplier=0,
                      allow_small_or_imprecise_dtypes=True).then_inc(s_iota, 1)

            def held(s, v):
                pool.wait_ge(s, v)
                pool.nop(nofuse=True)

            held(s_padw, 16 * NI)
            with pool.Fori(0, NIS) as i:
                for k in range(SETS):
                    held(s_at[k], (i + 1) * 16)
                    held(s_ms[k], i + 1)
                    held(s_pl[k], i + 1)
                    for j in range(GT):
                        pool.indirect_dma_start(
                            payload_rows, bass.IndirectOffsetOnAxis(ap=place_slot[:, k, j:j + 1], axis=0),
                            edges[0:EP, k, j, :], None).then_inc(s_sc[k], 16)

            def gather(loop, nth_index, nth, tbl, width):
                held(s_tab, 16 * (nth + 1))
                with pool.Fori(0, NI) as i:
                    for k in range(SETS):
                        held(s_ix[k], i + (1 + nth_index * NI))
                        held(s_used[k], i + (1 + loop * NI))
                        for j in range(GT):
                            pool.indirect_dma_start(
                                gat[:, k, j, 0:width], None, tbl,
                                bass.IndirectOffsetOnAxis(ap=index[:, k, j:j + 1], axis=0)).then_inc(s_g[k], 16)

            gather(0, 0, 0, table[0], D)
            gather(1, 1, 1, table[1], D)
            held(s_padm, 16 * NI)
            with pool.Fori(0, NI) as i:
                for k in range(SETS):
                    held(s_ix[k], i + (1 + 2 * NI))
                    held(s_msg[k], i + 1)
                    for j in range(GT):
                        pool.indirect_dma_start(
                            message_rows, bass.IndirectOffsetOnAxis(ap=index[:, k, j:j + 1], axis=0),
                            msg[:, k, j, :], None, bounds_check=ROWS - 1, oob_is_err=False).then_inc(s_msc[k], 16)
            gather(4, 3, 2, table3, 2 * D)

        @block.vector
        def _(dve):
            links = [0]

            def link(ins):
                links[0] += 1
                ins.then_inc(s_vl, 1)
                dve.wait_ge(s_vl, links[0])

            def wide(s):
                return s.unsqueeze(2).broadcast_to([BP, NB, D])

            dve.wait_ge(s_iota, 3)
            link(dve.tensor_copy(iota[:, :], iota_i[:, :]))
            link(dve.tensor_scalar(ident[:, :], iota[:, :], part[:, 0:1], None, ALU.is_equal))
            link(dve.tensor_scalar(upper[:, :], iota[:, :], part[:, 0:1], None, ALU.is_gt))
            link(dve.memset(ones[:, :], 1.0))
            link(dve.memset(zrow[:, :], 0.0))
            dve.memset(hT[D:D + 1, :], 1.0).then_inc(s_const, 1)
            link(dve.memset(pad_pay[:, :, :], 0.0))
            link(dve.memset(pad_msg[:, :, :], 0.0))
            link(dve.memset(pad_pay[:, :, 1:2], -1.0))
            link(dve.memset(pad_pay[:, :, 3:4], float(ROWS)))
            link(dve.memset(pad_pay[:, :, 4:5], -1.0))
            dve.memset(pad_msg[:, :, D:D + 1], -1.0).then_inc(s_pad, 2)

            roots = [0]

            def inverse_root(scale, eps):
                v, s0, r, q = stat[:, 2, :], stat[:, 3, :], stat[:, 4, :], stat[:, 5, :]
                roots[0] += 1
                dve.tensor_scalar(v, v, scale, eps, ALU.mult, ALU.add).then_inc(s_var, 1)
                dve.wait_ge(s_sd, roots[0])
                dve.wait_ge(s_var, roots[0])
                link(dve.reciprocal(r, s0))
                link(dve.tensor_tensor(q, v, r, ALU.mult))
                link(dve.tensor_tensor(q, q, s0, ALU.add))
                link(dve.tensor_scalar(r, q, 0.5, None, ALU.mult))
                link(dve.reciprocal(q, r))
                return q

            def centre(src):
                link(dve.tensor_reduce(stat[:, 0, :], src, AX_X, ALU.add))
                link(dve.tensor_scalar(stat[:, 1, :], stat[:, 0, :], 1.0 / D, None, ALU.mult))
                link(dve.tensor_tensor(tmp[:, :, :], src, wide(stat[:, 1, :]), ALU.subtract))
                link(dve.tensor_tensor(agg[:, :, 0:D], tmp[:, :, :], tmp[:, :, :], ALU.mult))
                link(dve.tensor_reduce(stat[:, 2, :], agg[:, :, 0:D], AX_X, ALU.add))

            def layernorm_relu():
                centre(x[:, :, :])
                q = inverse_root(1.0 / D, 1e-5)
                link(dve.tensor_tensor(tmp[:, :, :], tmp[:, :, :], wide(q), ALU.mult))
                dve.tensor_scalar(h[:, :, :], tmp[:, :, :], 0.0, None, ALU.max).then_inc(s_h, 1)

            dve.wait_ge(s_x, 16)
            layernorm_relu()

            link(dve.memset(ones_row, 1.0))

            def rank(n, loc, row_out):
                link(dve.tensor_scalar(blk, key, float(BP), None, ALU.is_ge))
                for b in range(2, NB):
                    link(dve.scalar_tensor_tensor(out=blk, in0=key, scalar=float(BP * b), in1=blk,
                                                  op0=ALU.is_ge, op1=ALU.add))
                link(dve.scalar_tensor_tensor(out=loc, in0=blk, scalar=-float(BP), in1=key,
                                              op0=ALU.mult, op1=ALU.add))
                for b in range(NB):
                    link(dve.tensor_scalar(mask, blk, float(b), None, ALU.is_equal, ALU.add,
                                           accum_out=count[:, b:b + 1]))
                dve.tensor_copy(need[:, :], count[:, :]).then_inc(s_cnt, 1)
                dve.wait_ge(s_pre, n + 1)
                link(dve.tensor_scalar(need_i[:, :], psum[0:EP, 0, 32:32 + NB], 127.0, None, ALU.add))
                link(dve.tensor_scalar(need_i[:, :], need_i[:, :], 7, None, ALU.logical_shift_right))
                link(dve.tensor_copy(need[:, :], need_i[:, :]))
                link(dve.tensor_tensor_scan(ends[:, :], ones_row[:, 0:NB], need[:, :], 0.0, ALU.mult, ALU.add))
                link(dve.tensor_tensor(base[:, :], ends[:, :], need[:, :], ALU.subtract))
                link(dve.tensor_scalar(base[:, :], base[:, :], 128.0, -1.0, ALU.mult, ALU.add))
                link(dve.tensor_tensor(base[:, :], base[:, :], psum[0:EP, 0, 0:NB], ALU.add))
                link(dve.memset(pos, 0.0))
                for b in range(NB):
                    link(dve.tensor_scalar(mask, blk, float(b), None, ALU.is_equal))
                    link(dve.tensor_tensor_scan(csum, ones_row, mask, base[:, b:b + 1], ALU.mult, ALU.add))
                    link(dve.tensor_tensor(prod, mask, csum, ALU.mult))
                    link(dve.tensor_tensor(pos, pos, prod, ALU.add))
                link(dve.tensor_copy(row_i, pos))
                link(dve.tensor_scalar(tile_i, row_i, 7, None, ALU.logical_shift_right))
                link(dve.tensor_scalar(row_i, row_i, 127, None, ALU.bitwise_and))
                link(dve.tensor_copy(mask, row_i))
                link(dve.tensor_copy(prod, tile_i))
                return dve.scalar_tensor_tensor(out=row_out, in0=mask, scalar=float(T), in1=prod,
                                                op0=ALU.mult, op1=ALU.add)

            def tile_columns(dst, step, jump):
                link(dve.memset(tile_row, 0.0))
                for b in range(NB - 1):
                    s = step + (jump if (b + 1) % PER_BANK == 0 else 0)
                    link(dve.tensor_scalar(tile_step, iota_t[0:1, :], ends[0:1, b:b + 1], float(s), ALU.is_ge, ALU.mult))
                    link(dve.tensor_tensor(tile_row, tile_row, tile_step, ALU.add))
                return dve.tensor_copy(dst[:, :], tile_row)

            dve.wait_ge(s_key, 48)
            link(dve.tensor_copy(meta[:, :, 2], prod))
            link(dve.tensor_copy(meta[:, :, 0], csum.bitcast(I32)))
            link(dve.tensor_copy(mask, key.bitcast(I32)))
            link(dve.tensor_copy(key, mask))
            link(rank(0, meta[:, :, 1], place))
            link(tile_columns(acc_d, AW, 512 - PER_BANK * AW))
            link(tile_columns(sup_d, D, 0))
            link(dve.memset(blk_t[:, :], 0.0))
            for b in range(NB - 1):
                link(dve.scalar_tensor_tensor(out=blk_t[:, :], in0=iota_t[:, :], scalar=ends[0:BP, b:b + 1],
                                              in1=blk_t[:, :], op0=ALU.is_ge, op1=ALU.add))
            link(dve.tensor_copy(key, meta[:, :, 0]))
            link(rank(1, meta[:, :, 4], meta[:, :, 3]))
            tile_columns(acc_s, AW, 512 - PER_BANK * AW).then_inc(s_meta, 1)

            with dve.Fori(0, NIS) as i:
                for k in range(SETS):
                    dve.wait_ge(s_fr[k], i + 1)
                    dve.tensor_copy(place_slot[:, k, :], place[:, bass.ds(i * BODY + k * GT, GT)]).then_inc(s_pl[k], 1)

            for k in range(SETS):
                dve.wait_ge(s_sc[k], 16 * GT * NIS)
            dve.memset(sT[D:D + 1, :], 1.0).then_inc(s_norm, 1)

            def one_hot(k, i, loop, group, column, weight=None):
                dve.wait_ge(s_ed[k], (i + (1 + loop * NI)) * 16)
                dve.wait_ge(s_used[k], i + (1 + loop * NI))
                for j in range(GT):
                    if weight is None:
                        ins = dve.tensor_scalar(hot[:, k, j, :], iota[:, 0:BP], group[:, k, j, column:column + 1],
                                                None, ALU.is_equal)
                    else:
                        ins = dve.tensor_scalar(hot[:, k, j, :], iota[:, 0:BP], group[:, k, j, column:column + 1],
                                                weight(j), ALU.is_equal, ALU.mult)
                ins.then_inc(s_hot[k], 1)

            def indices(k, i, loop, nth, column):
                dve.wait_ge(s_ed[k], (i + (1 + loop * NI)) * 16)
                dve.wait_ge(s_used[k], i + (1 + loop * NI))
                dve.tensor_copy(index[:, k, :], edges[:, k, :, column]).then_inc(s_ix[k], 1)

            with dve.Fori(0, NI) as i:
                for k in range(SETS):
                    indices(k, i, 0, 0, 0)
                    one_hot(k, i, 0, edges, 1)
                    dve.wait_ge(s_hot[k], i + 1)
                    dve.tensor_scalar(pen[:, k, :, :], hot[:, k, :, :], BIG, -BIG, ALU.mult, ALU.add).then_inc(s_pen[k], 1)
                    dve.wait_ge(s_vt[k], i + 1)
                    dve.wait_ge(s_exp[k], 2 * i + 1)
                    dve.tensor_reduce(nmx[:, k, :], psum[0:BP, 5 + k % 2, :].rearrange("p (j e) -> p j e", j=GT),
                                      AX_X, ALU.max, negate=True).then_inc(s_mx[k], 1)
                    dve.wait_ge(s_mx[k], i + 1)
                    dve.tensor_copy(nmx_all[:, bass.ds(i * BODY + k * GT, GT)], nmx[:, k, :]).then_inc(s_vl, 1)
            links[0] += NI * SETS
            dve.wait_ge(s_vl, links[0])

            def divide_by_std(n):
                centre(z[:, :, :])
                q = inverse_root(1.0 / (D - 1), 0.0)
                return dve.tensor_tensor(n, z[:, :, :], wide(q), ALU.mult)

            def after(step):
                dve.wait_ge(s_ev, FIRST[step] + SIZE[step])

            for k in range(SETS):
                dve.wait_ge(s_exp[k], 2 * NI + 1)
            link(dve.memset(nmx_full, 0.0))
            for b in range(NB):
                link(dve.tensor_scalar(seg_tmp, blk_t[:, :], float(b), BIG, ALU.not_equal, ALU.mult))
                link(dve.tensor_tensor(seg_tmp, seg_tmp, nmx_all, ALU.add))
                link(dve.tensor_reduce(seg_m[:, b:b + 1], seg_tmp, AX_X, ALU.min))
                link(dve.tensor_scalar(seg_tmp, blk_t[:, :], float(b), seg_m[:, b:b + 1], ALU.is_equal, ALU.mult))
                link(dve.tensor_tensor(nmx_full, nmx_full, seg_tmp, ALU.add))
            dve.tensor_tensor(nmx_full, nmx_full, nmx_all, ALU.subtract).then_inc(s_seg, 1)
            dve.wait_ge(s_segx, 1)
            link(dve.tensor_tensor(den_all, den_all, nmx_full, ALU.mult))
            for b in range(NB):
                link(dve.tensor_scalar(seg_tmp, blk_t[:, :], float(b), None, ALU.is_equal))
                link(dve.tensor_tensor(seg_tmp, seg_tmp, den_all, ALU.mult))
                link(dve.tensor_reduce(seg_d[:, b:b + 1], seg_tmp, AX_X, ALU.add))
            link(dve.tensor_scalar(seg_m[:, :], seg_m[:, :], BIG / 2, None, ALU.is_lt))
            link(dve.tensor_tensor(seg_d[:, :], seg_d[:, :], seg_m[:, :], ALU.mult))
            link(dve.tensor_scalar(share[:, :], seg_d[:, :], 1e-30, None, ALU.max))
            link(dve.reciprocal(seg_m[:, :], share[:, :]))
            link(dve.tensor_tensor(share[:, :], seg_d[:, :], seg_m[:, :], ALU.mult))

            after("z0")
            divide_by_std(h[:, :, :]).then_inc(s_h, 1)

            with dve.Fori(0, NI) as i:
                for k in range(SETS):
                    indices(k, i, 1, 1, 0)
                    one_hot(k, i, 1, edges, 1)
            after("z1")
            link(divide_by_std(z[:, :, :]))
            link(dve.tensor_tensor(x[:, :, :], x[:, :, :], z[:, :, :], ALU.add))
            layernorm_relu()

            after("y")
            link(dve.tensor_tensor(z[:, :, :], z[:, :, :], wide(share[:, :]), ALU.mult))
            link(dve.tensor_tensor(x[:, :, :], x[:, :, :], z[:, :, :], ALU.add))
            layernorm_relu()

            with dve.Fori(0, NI) as i:
                for k in range(SETS):
                    indices(k, i, 2, 2, 3)
                    dve.tensor_copy(msg[:, k, :, D], edges[:, k, :, 4])
                    one_hot(k, i, 2, edges, 1, lambda j: edges[:, k, j, 2:3])
                    dve.wait_ge(s_sup[k], i + 1)
                    dve.tensor_copy(msg[:, k, :, 0:D],
                                    psum[:, k, 0:GT * D].rearrange("p (j f) -> p j f", j=GT)).then_inc(s_msg[k], 1)

            with dve.Fori(0, NI) as i:
                for k in range(SETS):
                    one_hot(k, i, 3, msg, D)
            dve.wait_ge(s_agg, 3)
            link(dve.tensor_tensor(x[:, :, :], x[:, :, :], agg[:, :, 0:D], ALU.add))
            link(dve.tensor_tensor(x[:, :, :], x[:, :, :], l2b[:, :].unsqueeze(1).broadcast_to([BP, NB, D]), ALU.add))
            layernorm_relu()

            link(dve.tensor_scalar(gw2[:, :], gw2[:, :], 0.5, None, ALU.mult))
            link(dve.tensor_scalar(gb2[:, :], gb2[:, :], 0.5, None, ALU.mult))
            for k in range(SETS):
                dve.wait_ge(s_used[k], 1 + 4 * NI)
            link(dve.memset(gel[:, :, :, 0, D:D + 1].rearrange("p k j n -> p (k j) n"), 1.0))
            def add_parts(i, k):
                dve.wait_ge(s_g[k], (i + (1 + 2 * NI)) * (16 * GT))
                dve.wait_ge(s_pre3[k], i + 1)
                for half in range(2):
                    ins = dve.tensor_tensor(
                        gat[:, k, 2 * half:2 * half + 2, :], gat[:, k, 2 * half:2 * half + 2, :],
                        psum[:, 6 + half, 0:4 * D].rearrange("p (j f) -> p j f", j=2), ALU.add)
                ins.then_inc(s_hid[k], 1)

            def edge_step(i, k, last=False):
                if not last or k < 2:
                    i2, k2 = (i, k + 2) if k < 2 else (i + 1, k - 2)
                    indices(k2, i2, 4, 3, 0)
                dve.wait_ge(s_gel[k], i + 1)
                dve.tensor_tensor(gprod[:, :, :], gel[:, k, :, 1, 0:D],
                                  gw2[:, :].unsqueeze(1).broadcast_to([128, GT, D]), ALU.mult).then_inc(s_prod, 1)
                dve.wait_ge(s_prod, i * SETS + (k + 1))
                dve.tensor_reduce(gsum[:, k, :], gprod[:, :, :], AX_X, ALU.add).then_inc(s_dot[k], 1)
                if not last or k < SETS - 1:
                    add_parts(*following(i, k))
                dve.wait_ge(s_gate[k], i + 1)
                dve.tensor_scalar(gate[:, k, :], gsum[:, k, :], 0.5, 0.5, ALU.mult, ALU.add).then_inc(s_gst, 1)
                dve.wait_ge(s_gst, i * SETS + (k + 1))
                one_hot(k, i, 4, edges, 1, lambda j: gate[:, k, j:j + 1])

            indices(0, 0, 4, 3, 0)
            indices(1, 0, 4, 3, 0)
            add_parts(0, 0)
            with dve.Fori(0, NI - 1) as i:
                for k in range(SETS):
                    edge_step(i, k)
            for k in range(SETS):
                edge_step(NI - 1, k, last=True)

            dve.wait_ge(s_mm, FIRST["msgT"] + SIZE["msgT"])
            dve.memset(aT[D:D + 1, :], 1.0).then_inc(s_norm, 1)
            after("up")
            link(dve.tensor_tensor(z[:, :, :], z[:, :, :], h[:, :, :], ALU.add))
            centre(z[:, :, :])
            q = inverse_root(1.0 / D, 1e-5)
            link(dve.tensor_tensor(tmp[:, :, :], tmp[:, :, :], wide(q), ALU.mult))
            link(dve.tensor_tensor(tmp[:, :, :], tmp[:, :, :], ln_g[:, :].unsqueeze(1).broadcast_to([BP, NB, D]), ALU.mult))
            link(dve.tensor_tensor(tmp[:, :, :], tmp[:, :, :], ln_b[:, :].unsqueeze(1).broadcast_to([BP, NB, D]), ALU.add))
            dve.tensor_tensor(z[:, :, :], x[:, :, :], tmp[:, :, :], ALU.add).then_inc(s_res, 1)

        @block.scalar
        def _(act):
            roots = [0]

            def root():
                act.wait_ge(s_var, roots[0] + 1)
                act.activation(stat[:, 3, :], stat[:, 2, :], ACT.Sqrt).then_inc(s_sd, 1)
                roots[0] += 1

            def evacuate(step, dst, src, func=ACT.Copy):
                for j in range(SIZE[step]):
                    g = FIRST[step] + j
                    act.wait_ge(s_mm, g + 1)
                    act.activation(dst(j), src(j, psum[:, node_bank(g), :]), func).then_inc(s_ev, 1)

            def turned(to, rows=D):
                return (lambda j: to[0:rows, 4 * BP * j:min(4 * BP * (j + 1), N)],
                        lambda j, bank: bank[0:rows, 0:min(4 * BP, N - 4 * BP * j)])

            def blocks(to):
                return (lambda j: to[:, 5 * j:5 * j + 5, :].rearrange("p b f -> p (b f)"),
                        lambda j, bank: bank[0:BP, 0:5 * D])

            tab_b = tab[:, 0:NB * D].rearrange("p (b f) -> p b f", f=D)

            def aggregate(loop, n):
                for k in range(SETS):
                    act.wait_ge(s_used[k], 1 + (loop + 1) * NI)
                for j in range(5):
                    ins = act.activation(agg[:, 5 * j:5 * j + 5, :].rearrange("p b f -> p (b f)"),
                                         psum[0:BP, j, 0:5 * AW], ACT.Copy)
                ins.then_inc(s_agg, 1)

            root()
            evacuate("h0T", *turned(hT))
            evacuate("tab0", *blocks(tab_b))

            act.wait_ge(s_meta, 1)
            with act.Fori(0, NIS) as i:
                for k in range(SETS):
                    act.wait_ge(s_fr[k], i + 1)
                    act.activation(edges[0:EP, k, :, 0:5], meta[:, bass.ds(i * BODY + k * GT, GT), :],
                                   ACT.Copy).then_inc(s_ms[k], 1)

            evacuate("self0", *turned(sT))

            act.wait_ge(s_padm, 16 * NI)
            for k in range(SETS):
                act.sem_inc(s_exp[k], 1)
            with act.Fori(0, NI) as i:
                for k in range(SETS):
                    act.wait_ge(s_pen[k], i + 1)
                    for j in range(GT):
                        ins = act.activation(val[:, k, j, :], pen[:, k, j, :], ACT.Identity, bias=edges[:, k, j, 2:3])
                    ins.then_inc(s_val[k], 1)
                    act.wait_ge(s_mx[k], i + 1)
                    for j in range(GT):
                        at = psum[0:BP, 5 + k % 2, 128 * j:128 * j + 128]
                        ins = act.activation(at, at, ACT.Exp,
                                             bias=nmx[:, k, j:j + 1], accum_out=den[:, k, j:j + 1])
                    ins.then_inc(s_exp[k], 1)
                    act.wait_ge(s_exp[k], 2 * i + 2)
                    act.activation(den_all[:, bass.ds(i * BODY + k * GT, GT)], den[:, k, :], ACT.Copy).then_inc(s_exp[k], 1)

            aggregate(0, 1)
            evacuate("agg0T", *turned(aT))
            evacuate("z0", *blocks(z))
            act.wait_ge(s_seg, 1)
            act.activation(nmx_full, nmx_full, ACT.Exp).then_inc(s_segx, 1)
            root()
            evacuate("h1T", *turned(hT))
            act.wait_ge(s_tab, 16)
            evacuate("tab1", *blocks(tab_b))
            evacuate("self1", *turned(sT))
            aggregate(1, 2)
            evacuate("agg1T", *turned(aT))
            evacuate("z1", *blocks(z))
            root()
            root()
            evacuate("h2T", *turned(hT))
            evacuate("y", *blocks(z), func=ACT.Relu)
            root()
            evacuate("h3T", *turned(hT))
            act.wait_ge(s_tab, 32)
            evacuate("sup", *blocks(tab_b))

            with act.Fori(0, NI) as i:
                for k in range(SETS):
                    act.wait_ge(s_ht[k], i + 1)
                    act.activation(hotT[:, k, :], psum[0:BP, 5 + k % 2, :], ACT.Copy).then_inc(s_hte[k], 1)

            aggregate(3, 3)
            root()
            evacuate("h4T", *turned(hT))
            evacuate("tab3",
                     lambda j: tab[:, 4 * D * j:min(4 * D * (j + 1), 2 * D * NB)],
                     lambda j, bank: bank[0:BP, 0:min(4 * D, 2 * D * (NB - 2 * j))])

            def turn_attr(i, k):
                act.wait_ge(s_attT[k], i + 1)
                act.activation(attrT[:, k, :], psum[0:DE, 5, :], ACT.Copy).then_inc(s_atte[k], 1)

            def hidden(i, k):
                act.wait_ge(s_hid[k], i + 1)
                act.activation(gel[:, k, :, :, 0:D], gat[:, k, :, :].rearrange("p j (s f) -> p j s f", s=2),
                               ACT.Gelu).then_inc(s_gel[k], 1)

            def edge_step(i, k, last=False):
                if not last or k < SETS - 1:
                    turn_attr(*following(i, k))
                act.wait_ge(s_dot[k], i + 1)
                act.activation(gsum[:, k, :], gsum[:, k, :], ACT.Tanh, bias=gb2[:, 0:1]).then_inc(s_gate[k], 1)
                if not last or k < SETS - 1:
                    hidden(*following(i, k))

            turn_attr(0, 0)
            hidden(0, 0)
            with act.Fori(0, NI - 1) as i:
                for k in range(SETS):
                    edge_step(i, k)
            for k in range(SETS):
                edge_step(NI - 1, k, last=True)

            aggregate(4, 4)
            evacuate("agg3T", *turned(aT, D + 1))
            evacuate("msgT", *turned(sT))
            act.wait_ge(s_norm, 2)
            evacuate("uT", *turned(aT), func=ACT.Gelu)
            evacuate("up", *blocks(z))
            root()

        @block.tensor
        def _(pe):
            def open_group(g):
                if g >= 3:
                    pe.wait_ge(s_ev, g - 2)
                return psum[:, node_bank(g), :]

            def chunk(j):
                return 4 * BP * j, min(4 * BP, N - 4 * BP * j)

            def transpose_blocks(step, src, rows=D):
                for j in range(SIZE[step]):
                    bank = open_group(FIRST[step] + j)
                    for q in range(min(4, NB - 4 * j)):
                        ins = pe.transpose(bank[0:rows, BP * q:BP * q + BP], src[:, 4 * j + q, 0:rows], ident[0:BP, 0:BP])
                    ins.then_inc(s_mm, 1)

            def to_nodes(step, terms):
                for j in range(SIZE[step]):
                    bank = open_group(FIRST[step] + j)
                    for q in range(5):
                        b = 5 * j + q
                        for m, (lhs, rows, w) in enumerate(terms):
                            ins = pe.matmul(bank[0:BP, D * q:D * q + D], lhs[0:rows, BP * b:BP * b + BP],
                                            wt[0:rows, WI[w], :], start=(m == 0), stop=(m == len(terms) - 1))
                    ins.then_inc(s_mm, 1)

            def to_features(step, terms):
                for j in range(SIZE[step]):
                    bank = open_group(FIRST[step] + j)
                    lo, n = chunk(j)
                    for m, (rhs, rows, w) in enumerate(terms):
                        ins = pe.matmul(bank[0:D, 0:n], wt[0:rows, WI[w], :], rhs[0:rows, lo:lo + n],
                                        start=(m == 0), stop=(m == len(terms) - 1))
                    ins.then_inc(s_mm, 1)

            def evacuated(step):
                pe.wait_ge(s_ev, FIRST[step] + SIZE[step])

            def zero_sums():
                for j in range(5):
                    pe.matmul(psum[0:BP, j, :], zrow[:, 0:BP], zrow[:, :], start=True, stop=True)

            def add_tile(k, j, column, rhs):
                width = rhs.shape[-1]
                return pe.matmul(acc[:, bass.ds(column, width)], hot[:, k, j, :], rhs,
                                 start=False, stop=True, skip_group_check=True)

            def column(tbl, i, k, j, top):
                return pe.value_load(tbl[0:1, bass.ds(i * BODY + (k * GT + j), 1)], min_val=0, max_val=top)

            ACC_TOP = 4 * 512 + 4 * AW
            SUP_TOP = (NB - 1) * D

            pe.wait_ge(s_const, 1)
            pe.wait_ge(s_w, 16 * WEIGHT_LOADS)
            pe.wait_ge(s_h, 1)
            transpose_blocks("h0T", h)
            evacuated("h0T")
            to_nodes("tab0", [(hT, D + 1, "W0_0")])
            for n in range(2):
                pe.wait_ge(s_cnt, n + 1)
                pe.matmul(psum[0:EP, 0, 0:NB], upper[0:EP, 0:EP], count[:, :], start=True, stop=True)
                pe.matmul(psum[0:EP, 0, 32:32 + NB], ones[0:EP, 0:EP], count[:, :], start=True, stop=True).then_inc(s_pre, 1)

            for k in range(SETS):
                pe.wait_ge(s_sc[k], 16 * GT * NIS)
            to_features("self0", [(hT, D + 1, "W1_0")])

            for k in range(SETS):
                pe.sem_inc(s_used[k], 1)
            evacuated("self0")
            zero_sums()
            with pe.Fori(0, NI) as i:
                for k in range(SETS):
                    pe.wait_ge(s_val[k], i + 1)
                    pe.wait_ge(s_exp[(k + 2) % 4], 2 * i + (1 if k < 2 else 2))
                    for j in range(GT):
                        ins = pe.transpose(psum[0:BP, 5 + k % 2, 128 * j:128 * j + 128], val[:, k, j, :], ident[:, :])
                    ins.then_inc(s_vt[k], 1)
                    pe.wait_ge(s_hot[k], i + 1)
                    pe.wait_ge(s_g[k], (i + 1) * (16 * GT))
                    for j in range(GT):
                        ins = add_tile(k, j, column(acc_d, i, k, j, ACC_TOP), gat[:, k, j, 0:D])
                    ins.then_inc(s_used[k], 1)
            pe.wait_ge(s_agg, 1)
            for k in range(SETS):
                pe.wait_ge(s_exp[k], 2 * NI + 1)
            transpose_blocks("agg0T", agg)
            evacuated("agg0T")
            pe.wait_ge(s_norm, 1)
            to_nodes("z0", [(sT, D + 1, "W2a_0"), (aT, D, "W2b_0")])
            pe.wait_ge(s_h, 2)
            transpose_blocks("h1T", h)
            evacuated("h1T")
            to_nodes("tab1", [(hT, D + 1, "W0_1")])
            to_features("self1", [(hT, D + 1, "W1_1")])

            evacuated("self1")
            zero_sums()
            with pe.Fori(0, NI) as i:
                for k in range(SETS):
                    pe.wait_ge(s_hot[k], i + (1 + NI))
                    pe.wait_ge(s_g[k], (i + (1 + NI)) * (16 * GT))
                    for j in range(GT):
                        ins = add_tile(k, j, column(acc_d, i, k, j, ACC_TOP), gat[:, k, j, 0:D])
                    ins.then_inc(s_used[k], 1)
            pe.wait_ge(s_agg, 2)
            transpose_blocks("agg1T", agg)
            evacuated("agg1T")
            to_nodes("z1", [(sT, D + 1, "W2a_1"), (aT, D, "W2b_1")])

            pe.wait_ge(s_h, 3)
            transpose_blocks("h2T", h)
            evacuated("h2T")
            to_nodes("y", [(hT, D + 1, "Wv")])

            pe.wait_ge(s_h, 4)
            transpose_blocks("h3T", h)
            evacuated("h3T")
            to_nodes("sup", [(hT, D, "Wl2")])
            evacuated("sup")
            with pe.Fori(0, NI) as i:
                for k in range(SETS):
                    pe.wait_ge(s_hot[k], i + (1 + 2 * NI))
                    for j in range(GT):
                        ins = pe.transpose(psum[0:BP, 5 + k % 2, 128 * j:128 * j + 128], hot[:, k, j, :], ident[:, :])
                    ins.then_inc(s_ht[k], 1)
                    pe.wait_ge(s_hte[k], i + 1)
                    for j in range(GT):
                        c = column(sup_d, i, k, j, SUP_TOP)
                        ins = pe.matmul(psum[:, k, D * j:D * j + D], hotT[:, k, 128 * j:128 * j + 128],
                                        tab[:, bass.ds(c, D)], start=True, stop=True)
                    ins.then_inc(s_sup[k], 1)
            for k in range(SETS):
                pe.wait_ge(s_msg[k], NI)
            zero_sums()
            with pe.Fori(0, NI) as i:
                for k in range(SETS):
                    pe.wait_ge(s_hot[k], i + (1 + 3 * NI))
                    pe.wait_ge(s_ed[k], (i + (1 + 3 * NI)) * 16)
                    for j in range(GT):
                        ins = add_tile(k, j, column(acc_s, i, k, j, ACC_TOP), msg[:, k, j, 0:D])
                    ins.then_inc(s_used[k], 1)

            pe.wait_ge(s_h, 5)
            transpose_blocks("h4T", h)
            evacuated("h4T")
            for j in range(SIZE["tab3"]):
                bank = open_group(FIRST["tab3"] + j)
                for q in range(min(2, NB - 2 * j)):
                    b = 2 * j + q
                    for half, w in enumerate(("mW1x", "gW1x")):
                        ins = pe.matmul(bank[0:BP, D * (2 * q + half):D * (2 * q + half) + D], hT[0:D + 1, BP * b:BP * b + BP],
                                        wt[0:D + 1, WI[w], :], start=True, stop=True)
                ins.then_inc(s_mm, 1)
            evacuated("tab3")
            zero_sums()
            def edge_part(i, k, waits=True):
                pe.wait_ge(s_ed[k], (i + (1 + 4 * NI)) * 16)
                for j in range(GT):
                    ins = pe.transpose(psum[0:DE, 5, 128 * j:128 * j + 128], edges[:, k, j, 5:PW], ident[:, :])
                ins.then_inc(s_attT[k], 1)
                pe.wait_ge(s_atte[k], i + 1)
                if waits:
                    pe.wait_ge(s_hid[(k - 1) % SETS], i + 1 if k else i)
                for j in range(GT):
                    ins = pe.matmul(psum[:, 6 + j // 2, 2 * D * (j % 2):2 * D * (j % 2) + 2 * D],
                                    attrT[:, k, 128 * j:128 * j + 128],
                                    wt[0:DE, WI["mW1e"]:WI["mW1e"] + 2, :].rearrange("p w f -> p (w f)"),
                                    start=True, stop=True)
                ins.then_inc(s_pre3[k], 1)

            def edge_step(i, k, last=False):
                if not last or k < SETS - 1:
                    edge_part(*following(i, k))
                pe.wait_ge(s_hot[k], i + (1 + 4 * NI))
                for j in range(GT):
                    ins = add_tile(k, j, column(acc_d, i, k, j, ACC_TOP), gel[:, k, j, 0, :])
                ins.then_inc(s_used[k], 1)

            edge_part(0, 0, waits=False)
            with pe.Fori(0, NI - 1) as i:
                for k in range(SETS):
                    edge_step(i, k)
            for k in range(SETS):
                edge_step(NI - 1, k, last=True)
            pe.wait_ge(s_agg, 4)
            transpose_blocks("agg3T", agg, D + 1)
            evacuated("agg3T")
            to_features("msgT", [(aT, D + 1, "mW2")])
            evacuated("msgT")
            to_features("uT", [(hT, D + 1, "uW1a"), (sT, D, "uW1b")])
            evacuated("uT")
            to_nodes("up", [(aT, D + 1, "uW2")])


_INS = ["x", "src", "dst", "edge_attr_32", "edge_weight", "L0_gnn_W0", "L0_gnn_b0", "L0_gnn_W1", "L0_gnn_b1",
        "L0_gnn_W2", "L0_gnn_b2", "L1_gnn_Wv", "L1_gnn_bv", "L2_gnn_weight", "L2_gnn_b",
        "L3_gnn_mW1", "L3_gnn_mb1", "L3_gnn_mW2", "L3_gnn_mb2", "L3_gnn_gW1", "L3_gnn_gb1", "L3_gnn_gW2",
        "L3_gnn_gb2", "L3_gnn_uW1", "L3_gnn_ub1", "L3_gnn_uW2", "L3_gnn_ub2", "L3_gnn_ln_g", "L3_gnn_ln_b"]


def kernel(**inputs):
    import numpy as _np
    import concourse.bacc as _bacc
    from concourse import mybir as _mybir
    from concourse.bass_utils import run_bass_kernel_spmd as _run

    nc = _bacc.Bacc("TRN2", target_bir_lowering=False, num_devices=1)
    arrays, aps = {}, {}
    for name in _INS:
        v = _np.ascontiguousarray(inputs[name])
        arrays[f"in_{name}_dram"] = v
        aps[name] = nc.dram_tensor(f"in_{name}_dram", v.shape, _mybir.dt.from_np(v.dtype), kind="ExternalInput").ap()
    out = nc.dram_tensor("out_0_dram", (N, D), _mybir.dt.float32, kind="ExternalOutput").ap()
    build(nc, aps, out)
    r = _run(nc, [arrays], core_ids=[0])
    return r.results[0]["out_0_dram"]
```

```python
from contextlib import ExitStack

import concourse.bass as bass
from concourse import mybir

ALU = mybir.AluOpType
ACT = mybir.ActivationFunctionType
AX_X = mybir.AxisListType.X
F32 = mybir.dt.float32
I32 = mybir.dt.int32
BF16 = mybir.dt.bfloat16

D = 96
DE = 32
NB = 25
BP = 125
N = NB * BP
EP, EC = 125, 800
E = EP * EC
T = 816
SETS, GT = 4, 4
BODY = SETS * GT
NI = T // BODY
NIS = EC // BODY
PW = 5 + DE
MW = D + 1
AW = D + 1
PER_BANK = 5
ROWS = 128 * T
BIG = 1e38
assert N == 3125 and E == 100000 and T * 128 >= E + 127 * NB and PER_BANK * AW <= 512

WEIGHTS = ["W0_0", "W0_1", "W1_0", "W1_1", "W2a_0", "W2a_1", "W2b_0", "W2b_1", "Wv", "Wl2",
           "mW1x", "gW1x", "mW1e", "gW1e", "mW2", "uW1a", "uW1b", "uW2"]
WEIGHT_LOADS = 39
WI = {n: i for i, n in enumerate(WEIGHTS)}

NODE_STEPS = [("h0T", 7), ("tab0", 5), ("self0", 7), ("agg0T", 7), ("z0", 5),
              ("h1T", 7), ("tab1", 5), ("self1", 7), ("agg1T", 7), ("z1", 5),
              ("h2T", 7), ("y", 5), ("h3T", 7), ("sup", 5),
              ("h4T", 7), ("tab3", 13), ("agg3T", 7), ("msgT", 7), ("uT", 7), ("up", 5)]
FIRST, SIZE = {}, {}
_n = 0
for _name, _k in NODE_STEPS:
    FIRST[_name], SIZE[_name] = _n, _k
    _n += _k


def following(i, k):
    return (i, k + 1) if k < SETS - 1 else (i + 1, 0)


def pipelined(eng, first, step, top=lambda i: None):
    first(0, 0)
    with eng.Fori(0, NI - 1) as i:
        v = top(i)
        for k in range(SETS):
            step(i, k, False, v)
    v = top(NI - 1)
    for k in range(SETS):
        step(NI - 1, k, k == SETS - 1, v)


def node_bank(g):
    return 5 + g % 3


def build(nc, a, out):
    ctx = ExitStack()
    with ctx:
        def sb(name, shape, dt=F32):
            return ctx.enter_context(nc.sbuf_tensor(name, shape, dt))

        def sem(name):
            return ctx.enter_context(nc.semaphore(name))

        payload = nc.dram_tensor("payload", (128, T * PW), F32, kind="Internal").ap()
        messages = nc.dram_tensor("messages", (128, T * MW), F32, kind="Internal").ap()
        payload_rows = payload.rearrange("p (t w) -> (p t) w", w=PW)
        message_rows = messages.rearrange("p (t w) -> (p t) w", w=MW)
        table = [nc.dram_tensor(f"table{d}", (N, D), F32, kind="Internal").ap() for d in range(2)]
        table3 = nc.dram_tensor("table3", (N, 3 * 2 * D), BF16, kind="Internal").ap()

        x = sb("x", [BP, NB, D])
        h = sb("h", [BP, NB, D])
        z = sb("z", [BP, NB, D])
        tmp = sb("tmp", [BP, NB, D])
        agg = sb("agg", [BP, NB, AW])
        tab = sb("tab", [BP, NB * 2 * D])
        hT = sb("hT", [D + 1, N])
        wt = sb("wt", [D + 1, len(WEIGHTS), D])
        region = sb("region", [128, 11600])
        meta = region[0:EP, 0:EC * 5].rearrange("p (c w) -> p c w", w=5)

        def sort_array(i):
            return region[0:EP, (5 + i) * EC:(6 + i) * EC]

        key, blk, pos, mask, csum, prod, ones_row = (sort_array(i) for i in range(7))
        place = sort_array(7).bitcast(I32)
        tile_i = sort_array(8).bitcast(I32)
        row_i = csum.bitcast(I32)
        sT = region[0:D + 1, 0:N]
        aT = region[0:D + 1, N:2 * N]
        nmx_all = region[0:BP, 2 * N:2 * N + T]
        den_all = region[0:BP, 2 * N + T:2 * N + 2 * T]
        blk_t = sb("blk_t", [BP, T])
        seg_tmp = region[0:BP, 2 * N + 2 * T:2 * N + 3 * T]
        nmx_full = region[0:BP, 2 * N + 3 * T:2 * N + 4 * T]
        place_slot = sb("place_slot", [EP, SETS, GT], I32)
        acc_d = sb("acc_d", [1, T], I32)
        acc_s = sb("acc_s", [1, T], I32)
        sup_d = sb("sup_d", [1, T], I32)
        tile_row = region[0:1, 13 * EC:13 * EC + T]
        tile_inc = region[0:1, 5 * EC:5 * EC + T]
        iota_i = sb("iota_i", [128, 128], I32)
        iota = sb("iota", [128, 128])
        part = sb("part", [128, 1])
        iota_t = sb("iota_t", [BP, T])
        ident = sb("ident", [128, 128])
        upper = sb("upper", [128, 128])
        ones = sb("ones", [128, 128])
        zrow = sb("zrow", [1, 512])
        count = sb("count", [EP, NB])
        base = sb("base", [EP, NB])
        need = sb("need", [EP, NB])
        need_i = sb("need_i", [EP, NB], I32)
        ends = sb("ends", [EP, NB])
        stat = sb("stat", [BP, 8, NB])
        seg_m = sb("seg_m", [BP, NB])
        seg_d = sb("seg_d", [BP, NB])
        share = sb("share", [BP, NB])
        l2b = sb("l2b", [BP, D])
        ln_g = sb("ln_g", [BP, D])
        ln_b = sb("ln_b", [BP, D])
        gw2 = sb("gw2", [128, D])
        gb2 = sb("gb2", [128, 1])
        pad_pay = sb("pad_pay", [128, 16, PW])
        edges = sb("edges", [128, SETS, GT, PW])
        index = sb("index", [128, SETS, GT], I32)
        gat = sb("gat", [128, SETS, GT, 3 * D])
        gat3 = gat[:, :, :, :].bitcast(BF16)
        hot = sb("hot", [128, SETS, GT, BP])
        work = sb("work", [128, 4096])
        pen = work[:, 0:2000].rearrange("p (k j n) -> p k j n", k=SETS, j=GT)
        val = work[:, 2048:4048].rearrange("p (k j n) -> p k j n", k=SETS, j=GT)
        hotT = work[0:BP, 0:2048].rearrange("p (k e) -> p k e", k=SETS)
        pad_msg = work[:, 2048:2048 + 16 * MW].rearrange("p (t w) -> p t w", w=MW)
        msg = work[:, 2048:2048 + BODY * MW].rearrange("p (k j n) -> p k j n", k=SETS, j=GT)
        gel = work[:, 0:BODY * 2 * (D + 1)].rearrange("p (k j s n) -> p k j s n", k=SETS, j=GT, s=2)
        nmx = sb("nmx", [BP, SETS, GT])
        den = sb("den", [BP, SETS, GT])
        tab_parts = region[0:BP, 0:NB * 3 * D].bitcast(BF16).rearrange("p (b s f) -> p b s f", b=NB, s=3)
        attrT = region[0:3 * DE, 0:SETS * GT * 64].bitcast(BF16).rearrange("p (k e) -> p k e", k=SETS)
        attr_parts = sb("attr_parts", [128, SETS, GT, 3, DE], BF16)
        attr_rest = sb("attr_rest", [128, SETS, GT, DE])
        we_parts = sb("we_parts", [3 * DE, 3, 2 * D], BF16)
        ident_b = sb("ident_b", [128, 128], BF16)
        gprod = region[:, 8400:8400 + GT * D].rearrange("p (j f) -> p j f", j=GT)
        gsum = sb("gsum", [128, SETS, GT])
        gate = sb("gate", [128, SETS, GT])
        psum = ctx.enter_context(nc.psum_tensor("psum", [128, 8, 512], F32))
        attr_bank = psum[0:3 * DE, 5, 0:GT * 64].bitcast(BF16)
        acc = psum[0:BP, 0:5, :].rearrange("p a b -> p (a b)")

        s_w = sem("weights_loaded")
        s_x = sem("x_loaded")
        s_key = sem("keys_loaded")
        s_iota = sem("iotas_made")
        s_const = sem("constants_made")
        s_pad = sem("pad_tiles_made")
        s_padw = sem("payload_pads_written")
        s_padm = sem("message_pads_written")
        s_vl = sem("vector_link")
        s_al = sem("scalar_link")
        s_var = sem("variance_ready")
        s_sd = sem("sqrt_ready")
        s_h = sem("h_ready")
        s_mm = sem("node_group_done")
        s_ev = sem("node_group_evacuated")
        s_tab = sem("table_stored")
        s_cnt = sem("bucket_counts_ready")
        s_pre = sem("bucket_prefix_ready")
        s_meta = sem("meta_ready")
        s_agg = sem("agg_evacuated")
        s_norm = sem("node_update_done")
        s_seg = sem("segment_exponent_ready")
        s_segx = sem("segment_exp_done")
        s_out = sem("out_stored")
        s_res = sem("result_ready")
        s_parts = sem("table3_parts_ready")
        s_sp = sem("attr_split_steps")

        def sems(name):
            return [sem(f"{name}{k}") for k in range(SETS)]

        s_fr = sems("slot_free")
        s_at = sems("attr_loaded")
        s_ms = sems("meta_in_slot")
        s_pl = sems("place_in_slot")
        s_sc = sems("payload_scattered")
        s_ed = sems("edges_loaded")
        s_ix = sems("index_ready")
        s_g = sems("rows_gathered")
        s_hot = sems("hot_ready")
        s_used = sems("group_used")
        s_pen = sems("penalty_ready")
        s_val = sems("masked_weights_ready")
        s_vt = sems("masked_weights_transposed")
        s_mx = sems("tile_max_ready")
        s_exp = sems("tile_exp_done")
        s_ht = sems("hot_transposed")
        s_hte = sems("hotT_evacuated")
        s_sup = sems("support_rows_ready")
        s_msg = sems("messages_ready")
        s_msc = sems("messages_scattered")
        s_attT = sems("attr_transposed")
        s_atte = sems("attrT_evacuated")
        s_atp = sems("attr_parts_ready")
        s_hid = sems("edge_hidden_ready")
        s_gel = sems("gelu_done")
        s_dot = sems("gate_dot_ready")
        s_gate = sems("tanh_ready")
        s_prod = sem("gate_products_ready")
        s_gst = sem("gate_steps")

        block = ctx.enter_context(nc.Block())

        @block.sync
        def _(sp):
            sp.dma_start(x[:, :, :], a["x"].rearrange("(b p) f -> p b f", p=BP)).then_inc(s_x, 16)
            sp.dma_start(key.bitcast(I32), a["dst"].rearrange("(p c) -> p c", p=EP)).then_inc(s_key, 16)
            sp.dma_start(csum.bitcast(I32), a["src"].rearrange("(p c) -> p c", p=EP)).then_inc(s_key, 16)
            sp.dma_start(prod, a["edge_weight"].rearrange("(p c) -> p c", p=EP)).then_inc(s_key, 16)

            def row(v):
                return v.rearrange("(o n) -> o n", o=1)

            def weight(name, w, b=None):
                sp.dma_start(wt[0:w.shape[0], WI[name], :], w).then_inc(s_w, 16)
                if b is not None:
                    sp.dma_start(wt[D:D + 1, WI[name], :], row(b)).then_inc(s_w, 16)

            for d in range(2):
                weight(f"W0_{d}", a["L0_gnn_W0"][d], a["L0_gnn_b0"][d])
                weight(f"W1_{d}", a["L0_gnn_W1"][d], a["L0_gnn_b1"][d])
                weight(f"W2a_{d}", a["L0_gnn_W2"][d, 0:D], a["L0_gnn_b2"][d])
                weight(f"W2b_{d}", a["L0_gnn_W2"][d, D:2 * D])
            weight("Wv", a["L1_gnn_Wv"], a["L1_gnn_bv"])
            weight("Wl2", a["L2_gnn_weight"])
            weight("mW1x", a["L3_gnn_mW1"][0:D], a["L3_gnn_mb1"])
            weight("gW1x", a["L3_gnn_gW1"][0:D], a["L3_gnn_gb1"])
            for part in range(3):
                at = slice(DE * part, DE * part + DE)
                sp.dma_start(wt[at, WI["mW1e"], :], a["L3_gnn_mW1"][D:D + DE]).then_inc(s_w, 16)
                sp.dma_start(wt[at, WI["gW1e"], :], a["L3_gnn_gW1"][D:D + DE]).then_inc(s_w, 16)
            weight("mW2", a["L3_gnn_mW2"], a["L3_gnn_mb2"])
            weight("uW1a", a["L3_gnn_uW1"][0:D], a["L3_gnn_ub1"])
            weight("uW1b", a["L3_gnn_uW1"][D:2 * D])
            weight("uW2", a["L3_gnn_uW2"], a["L3_gnn_ub2"])
            for dst, v in ((l2b, "L2_gnn_b"), (ln_g, "L3_gnn_ln_g"), (ln_b, "L3_gnn_ln_b")):
                sp.dma_start(dst[:, :], a[v].partition_broadcast(BP)).then_inc(s_w, 16)
            sp.dma_start(gw2[:, :], a["L3_gnn_gW2"].rearrange("n o -> (n o)").partition_broadcast(128)).then_inc(s_w, 16)
            sp.dma_start(gb2[:, :], a["L3_gnn_gb2"].partition_broadcast(128)).then_inc(s_w, 16)

            sp.wait_ge(s_pad, 2)
            pad_pay_flat = pad_pay[:, :, :].rearrange("p t w -> p (t w)")
            pad_msg_flat = pad_msg[:, :, :].rearrange("p t w -> p (t w)")
            with sp.Fori(0, NI) as i:
                sp.dma_start(payload[:, bass.ds(i * 16 * PW, 16 * PW)], pad_pay_flat).then_inc(s_padw, 16)
            with sp.Fori(0, NI) as i:
                sp.dma_start(messages[:, bass.ds(i * 16 * MW, 16 * MW)], pad_msg_flat).then_inc(s_padm, 16)

            tab96 = tab[:, 0:NB * D].rearrange("p (b f) -> p b f", f=D)
            sp.wait_ge(s_ev, FIRST["tab0"] + SIZE["tab0"])
            sp.dma_start(table[0].rearrange("(b p) f -> p b f", p=BP), tab96).then_inc(s_tab, 16)

            attr = a["edge_attr_32"].rearrange("(p c) f -> p c f", p=EP)

            def load_attr(i, k):
                sp.sem_inc(s_fr[k], 1)
                sp.dma_start(edges[0:EP, k, :, 5:PW], attr[:, bass.ds(i * BODY + k * GT, GT), :]).then_inc(s_at[k], 16)

            for k in range(SETS):
                load_attr(0, k)
            with sp.Fori(1, NIS) as i:
                for k in range(SETS):
                    sp.wait_ge(s_sc[k], i * (16 * GT))
                    load_attr(i, k)
            for k in range(SETS):
                sp.wait_ge(s_sc[k], 16 * GT * NIS)

            def load_group(i, k):
                sp.dma_start(edges[:, k, :, :].rearrange("p j w -> p (j w)"),
                             payload[:, bass.ds((i * BODY + k * GT) * PW, GT * PW)]).then_inc(s_ed[k], 16)

            def load_edges(loop):
                with sp.Fori(0, NI) as i:
                    for k in range(SETS):
                        sp.wait_ge(s_used[k], i + (1 + loop * NI))
                        load_group(i, k)

            load_edges(0)
            sp.wait_ge(s_ev, FIRST["tab1"] + SIZE["tab1"])
            sp.dma_start(table[1].rearrange("(b p) f -> p b f", p=BP), tab96).then_inc(s_tab, 16)
            load_edges(1)
            for k in range(SETS):
                sp.wait_ge(s_used[k], 1 + 2 * NI)
                load_group(0, k)
            with sp.Fori(1, NI) as i:
                for k in range(SETS):
                    sp.wait_ge(s_msc[k], i * (16 * GT))
                    sp.sem_inc(s_used[k], 1)
                    load_group(i, k)
            for k in range(SETS):
                sp.wait_ge(s_msc[k], 16 * GT * NI)
                sp.sem_inc(s_used[k], 1)
            with sp.Fori(0, NI) as i:
                for k in range(SETS):
                    sp.wait_ge(s_used[k], i + (1 + 3 * NI))
                    sp.dma_start(msg[:, k, :, :].rearrange("p j w -> p (j w)"),
                                 messages[:, bass.ds((i * BODY + k * GT) * MW, GT * MW)]).then_inc(s_ed[k], 16)
            sp.wait_ge(s_parts, 1)
            sp.dma_start(table3.rearrange("(b p) f -> p b f", p=BP),
                         tab_parts.rearrange("p b s f -> p b (s f)")).then_inc(s_tab, 16)
            load_edges(4)
            sp.wait_ge(s_res, 1)
            sp.dma_start(out.rearrange("(b p) f -> p b f", p=BP), z[:, :, :]).then_inc(s_out, 16)
            sp.wait_ge(s_out, 16)

        @block.gpsimd
        def _(pool):
            pool.iota(iota_i[:, :], pattern=[[1, 128]], base=0, channel_multiplier=0).then_inc(s_iota, 1)
            pool.iota(part[:, :], pattern=[[0, 1]], base=0, channel_multiplier=1,
                      allow_small_or_imprecise_dtypes=True).then_inc(s_iota, 1)
            pool.iota(iota_t[:, :], pattern=[[1, T]], base=0, channel_multiplier=0,
                      allow_small_or_imprecise_dtypes=True).then_inc(s_iota, 1)

            def held(s, v):
                pool.wait_ge(s, v)
                pool.nop(nofuse=True)

            held(s_padw, 16 * NI)
            with pool.Fori(0, NIS) as i:
                for k in range(SETS):
                    held(s_at[k], (i + 1) * 16)
                    held(s_ms[k], i + 1)
                    held(s_pl[k], i + 1)
                    for j in range(GT):
                        pool.indirect_dma_start(
                            payload_rows, bass.IndirectOffsetOnAxis(ap=place_slot[:, k, j:j + 1], axis=0),
                            edges[0:EP, k, j, :], None).then_inc(s_sc[k], 16)

            def gather(loop, nth_index, nth, tbl, dst):
                held(s_tab, 16 * (nth + 1))
                with pool.Fori(0, NI) as i:
                    for k in range(SETS):
                        held(s_ix[k], i + (1 + nth_index * NI))
                        held(s_used[k], i + (1 + loop * NI))
                        for j in range(GT):
                            pool.indirect_dma_start(
                                dst(k, j), None, tbl,
                                bass.IndirectOffsetOnAxis(ap=index[:, k, j:j + 1], axis=0)).then_inc(s_g[k], 16)

            gather(0, 0, 0, table[0], lambda k, j: gat[:, k, j, 0:D])
            gather(1, 1, 1, table[1], lambda k, j: gat[:, k, j, 0:D])
            held(s_padm, 16 * NI)
            with pool.Fori(0, NI) as i:
                for k in range(SETS):
                    held(s_ix[k], i + (1 + 2 * NI))
                    held(s_msg[k], i + 1)
                    for j in range(GT):
                        pool.indirect_dma_start(
                            message_rows, bass.IndirectOffsetOnAxis(ap=index[:, k, j:j + 1], axis=0),
                            msg[:, k, j, :], None, bounds_check=ROWS - 1, oob_is_err=False).then_inc(s_msc[k], 16)
            gather(4, 3, 2, table3, lambda k, j: gat3[:, k, j, :])

        @block.vector
        def _(dve):
            links = [0]

            def link(ins):
                links[0] += 1
                ins.then_inc(s_vl, 1)
                dve.wait_ge(s_vl, links[0])

            def wide(s):
                return s.unsqueeze(2).broadcast_to([BP, NB, D])

            dve.wait_ge(s_iota, 3)
            link(dve.tensor_copy(iota[:, :], iota_i[:, :]))
            link(dve.tensor_scalar(ident[:, :], iota[:, :], part[:, 0:1], None, ALU.is_equal))
            link(dve.tensor_scalar(upper[:, :], iota[:, :], part[:, 0:1], None, ALU.is_gt))
            link(dve.memset(ones[:, :], 1.0))
            link(dve.memset(zrow[:, :], 0.0))
            dve.memset(hT[D:D + 1, :], 1.0).then_inc(s_const, 1)
            link(dve.memset(pad_pay[:, :, :], 0.0))
            link(dve.memset(pad_msg[:, :, :], 0.0))
            link(dve.memset(pad_pay[:, :, 1:2], -1.0))
            link(dve.memset(pad_pay[:, :, 3:4], float(ROWS)))
            link(dve.memset(pad_pay[:, :, 4:5], -1.0))
            dve.memset(pad_msg[:, :, D:D + 1], -1.0).then_inc(s_pad, 2)

            roots = [0]

            def inverse_root(scale, eps):
                v, s0, r, q = stat[:, 2, :], stat[:, 3, :], stat[:, 4, :], stat[:, 5, :]
                roots[0] += 1
                dve.tensor_scalar(v, v, scale, eps, ALU.mult, ALU.add).then_inc(s_var, 1)
                dve.wait_ge(s_sd, roots[0])
                dve.wait_ge(s_var, roots[0])
                link(dve.reciprocal(r, s0))
                link(dve.tensor_tensor(q, v, r, ALU.mult))
                link(dve.tensor_tensor(q, q, s0, ALU.add))
                link(dve.tensor_scalar(r, q, 0.5, None, ALU.mult))
                link(dve.reciprocal(q, r))
                return q

            def centre(src):
                link(dve.tensor_reduce(stat[:, 0, :], src, AX_X, ALU.add))
                link(dve.tensor_scalar(stat[:, 1, :], stat[:, 0, :], 1.0 / D, None, ALU.mult))
                link(dve.tensor_tensor(tmp[:, :, :], src, wide(stat[:, 1, :]), ALU.subtract))
                link(dve.tensor_tensor(agg[:, :, 0:D], tmp[:, :, :], tmp[:, :, :], ALU.mult))
                link(dve.tensor_reduce(stat[:, 2, :], agg[:, :, 0:D], AX_X, ALU.add))

            def layernorm_relu():
                centre(x[:, :, :])
                q = inverse_root(1.0 / D, 1e-5)
                link(dve.tensor_tensor(tmp[:, :, :], tmp[:, :, :], wide(q), ALU.mult))
                dve.tensor_scalar(h[:, :, :], tmp[:, :, :], 0.0, None, ALU.max).then_inc(s_h, 1)

            dve.wait_ge(s_x, 16)
            layernorm_relu()

            link(dve.memset(ones_row, 1.0))

            def rank(n, loc, row_out):
                link(dve.tensor_scalar(blk, key, float(BP), None, ALU.is_ge))
                for b in range(2, NB):
                    link(dve.scalar_tensor_tensor(out=blk, in0=key, scalar=float(BP * b), in1=blk,
                                                  op0=ALU.is_ge, op1=ALU.add))
                link(dve.scalar_tensor_tensor(out=loc, in0=blk, scalar=-float(BP), in1=key,
                                              op0=ALU.mult, op1=ALU.add))
                for b in range(NB):
                    link(dve.tensor_scalar(mask, blk, float(b), None, ALU.is_equal, ALU.add,
                                           accum_out=count[:, b:b + 1]))
                dve.tensor_copy(need[:, :], count[:, :]).then_inc(s_cnt, 1)
                dve.wait_ge(s_pre, n + 1)
                link(dve.tensor_scalar(need_i[:, :], psum[0:EP, 0, 32:32 + NB], 127.0, None, ALU.add))
                link(dve.tensor_scalar(need_i[:, :], need_i[:, :], 7, None, ALU.logical_shift_right))
                link(dve.tensor_copy(need[:, :], need_i[:, :]))
                link(dve.tensor_tensor_scan(ends[:, :], ones_row[:, 0:NB], need[:, :], 0.0, ALU.mult, ALU.add))
                link(dve.tensor_tensor(base[:, :], ends[:, :], need[:, :], ALU.subtract))
                link(dve.tensor_scalar(base[:, :], base[:, :], 128.0, -1.0, ALU.mult, ALU.add))
                link(dve.tensor_tensor(base[:, :], base[:, :], psum[0:EP, 0, 0:NB], ALU.add))
                link(dve.memset(pos, 0.0))
                for b in range(NB):
                    link(dve.tensor_scalar(mask, blk, float(b), None, ALU.is_equal))
                    link(dve.tensor_tensor_scan(csum, ones_row, mask, base[:, b:b + 1], ALU.mult, ALU.add))
                    link(dve.tensor_tensor(prod, mask, csum, ALU.mult))
                    link(dve.tensor_tensor(pos, pos, prod, ALU.add))
                link(dve.tensor_copy(row_i, pos))
                link(dve.tensor_scalar(tile_i, row_i, 7, None, ALU.logical_shift_right))
                link(dve.tensor_scalar(row_i, row_i, 127, None, ALU.bitwise_and))
                link(dve.tensor_copy(mask, row_i))
                link(dve.tensor_copy(prod, tile_i))
                return dve.scalar_tensor_tensor(out=row_out, in0=mask, scalar=float(T), in1=prod,
                                                op0=ALU.mult, op1=ALU.add)

            def tile_columns(dst, step, jump):
                link(dve.memset(tile_row, 0.0))
                for b in range(NB - 1):
                    s = step + (jump if (b + 1) % PER_BANK == 0 else 0)
                    link(dve.tensor_scalar(tile_inc, iota_t[0:1, :], ends[0:1, b:b + 1], float(s), ALU.is_ge, ALU.mult))
                    link(dve.tensor_tensor(tile_row, tile_row, tile_inc, ALU.add))
                return dve.tensor_copy(dst[:, :], tile_row)

            dve.wait_ge(s_key, 48)
            link(dve.tensor_copy(meta[:, :, 2], prod))
            link(dve.tensor_copy(meta[:, :, 0], csum.bitcast(I32)))
            link(dve.tensor_copy(mask, key.bitcast(I32)))
            link(dve.tensor_copy(key, mask))
            link(rank(0, meta[:, :, 1], place))
            link(tile_columns(acc_d, AW, 512 - PER_BANK * AW))
            link(tile_columns(sup_d, D, 0))
            link(dve.memset(blk_t[:, :], 0.0))
            for b in range(NB - 1):
                link(dve.scalar_tensor_tensor(out=blk_t[:, :], in0=iota_t[:, :], scalar=ends[0:BP, b:b + 1],
                                              in1=blk_t[:, :], op0=ALU.is_ge, op1=ALU.add))
            link(dve.tensor_copy(key, meta[:, :, 0]))
            link(rank(1, meta[:, :, 4], meta[:, :, 3]))
            tile_columns(acc_s, AW, 512 - PER_BANK * AW).then_inc(s_meta, 1)

            with dve.Fori(0, NIS) as i:
                for k in range(SETS):
                    dve.wait_ge(s_fr[k], i + 1)
                    dve.tensor_copy(place_slot[:, k, :], place[:, bass.ds(i * BODY + k * GT, GT)]).then_inc(s_pl[k], 1)

            for k in range(SETS):
                dve.wait_ge(s_sc[k], 16 * GT * NIS)
            dve.memset(sT[D:D + 1, :], 1.0).then_inc(s_norm, 1)

            def one_hot(k, i, loop, group, column, weight=None):
                dve.wait_ge(s_ed[k], (i + (1 + loop * NI)) * 16)
                dve.wait_ge(s_used[k], i + (1 + loop * NI))
                for j in range(GT):
                    if weight is None:
                        ins = dve.tensor_scalar(hot[:, k, j, :], iota[:, 0:BP], group[:, k, j, column:column + 1],
                                                None, ALU.is_equal)
                    else:
                        ins = dve.tensor_scalar(hot[:, k, j, :], iota[:, 0:BP], group[:, k, j, column:column + 1],
                                                weight(j), ALU.is_equal, ALU.mult)
                ins.then_inc(s_hot[k], 1)

            def indices(k, i, loop, nth, column):
                dve.wait_ge(s_ed[k], (i + (1 + loop * NI)) * 16)
                dve.wait_ge(s_used[k], i + (1 + loop * NI))
                dve.tensor_copy(index[:, k, :], edges[:, k, :, column]).then_inc(s_ix[k], 1)

            def tile_prepare(i, k):
                indices(k, i, 0, 0, 0)
                one_hot(k, i, 0, edges, 1)
                dve.wait_ge(s_hot[k], i + 1)
                dve.tensor_scalar(pen[:, k, :, :], hot[:, k, :, :], BIG, -BIG, ALU.mult, ALU.add).then_inc(s_pen[k], 1)

            def tile_step(i, k, last, _):
                if not last:
                    tile_prepare(*following(i, k))
                dve.wait_ge(s_vt[k], i + 1)
                dve.wait_ge(s_exp[k], 2 * i + 1)
                dve.tensor_reduce(nmx[:, k, :], psum[0:BP, 5 + k % 2, :].rearrange("p (j e) -> p j e", j=GT),
                                  AX_X, ALU.max, negate=True).then_inc(s_mx[k], 1)
                dve.wait_ge(s_mx[k], i + 1)
                at = i * BODY + k * GT
                dve.tensor_copy(nmx_all[:, bass.ds(at, GT)], nmx[:, k, :]).then_inc(s_vl, 1)

            pipelined(dve, tile_prepare, tile_step)
            links[0] += NI * SETS
            dve.wait_ge(s_vl, links[0])

            def divide_by_std(n):
                centre(z[:, :, :])
                q = inverse_root(1.0 / (D - 1), 0.0)
                return dve.tensor_tensor(n, z[:, :, :], wide(q), ALU.mult)

            def after(step):
                dve.wait_ge(s_ev, FIRST[step] + SIZE[step])

            for k in range(SETS):
                dve.wait_ge(s_exp[k], 2 * NI + 1)
            link(dve.memset(nmx_full, 0.0))
            for b in range(NB):
                link(dve.tensor_scalar(seg_tmp, blk_t[:, :], float(b), BIG, ALU.not_equal, ALU.mult))
                link(dve.tensor_tensor(seg_tmp, seg_tmp, nmx_all, ALU.add))
                link(dve.tensor_reduce(seg_m[:, b:b + 1], seg_tmp, AX_X, ALU.min))
                link(dve.tensor_scalar(seg_tmp, blk_t[:, :], float(b), seg_m[:, b:b + 1], ALU.is_equal, ALU.mult))
                link(dve.tensor_tensor(nmx_full, nmx_full, seg_tmp, ALU.add))
            dve.tensor_tensor(nmx_full, nmx_full, nmx_all, ALU.subtract).then_inc(s_seg, 1)
            dve.wait_ge(s_segx, 1)
            link(dve.tensor_tensor(den_all, den_all, nmx_full, ALU.mult))
            for b in range(NB):
                link(dve.tensor_scalar(seg_tmp, blk_t[:, :], float(b), None, ALU.is_equal))
                link(dve.tensor_tensor(seg_tmp, seg_tmp, den_all, ALU.mult))
                link(dve.tensor_reduce(seg_d[:, b:b + 1], seg_tmp, AX_X, ALU.add))
            link(dve.tensor_scalar(seg_m[:, :], seg_m[:, :], BIG / 2, None, ALU.is_lt))
            link(dve.tensor_tensor(seg_d[:, :], seg_d[:, :], seg_m[:, :], ALU.mult))
            link(dve.tensor_scalar(share[:, :], seg_d[:, :], 1e-30, None, ALU.max))
            link(dve.reciprocal(seg_m[:, :], share[:, :]))
            link(dve.tensor_tensor(share[:, :], seg_d[:, :], seg_m[:, :], ALU.mult))

            after("z0")
            divide_by_std(h[:, :, :]).then_inc(s_h, 1)

            with dve.Fori(0, NI) as i:
                for k in range(SETS):
                    indices(k, i, 1, 1, 0)
                    one_hot(k, i, 1, edges, 1)
            after("z1")
            link(divide_by_std(z[:, :, :]))
            link(dve.tensor_tensor(x[:, :, :], x[:, :, :], z[:, :, :], ALU.add))
            layernorm_relu()

            after("y")
            link(dve.tensor_tensor(z[:, :, :], z[:, :, :], wide(share[:, :]), ALU.mult))
            link(dve.tensor_tensor(x[:, :, :], x[:, :, :], z[:, :, :], ALU.add))
            layernorm_relu()

            def message_prepare(i, k):
                indices(k, i, 2, 2, 3)
                dve.tensor_copy(msg[:, k, :, D], edges[:, k, :, 4])
                one_hot(k, i, 2, edges, 1, lambda j: edges[:, k, j, 2:3])

            def message_step(i, k, last, _):
                if not last:
                    message_prepare(*following(i, k))
                dve.wait_ge(s_sup[k], i + 1)
                dve.tensor_copy(msg[:, k, :, 0:D],
                                psum[:, k, 0:GT * D].rearrange("p (j f) -> p j f", j=GT)).then_inc(s_msg[k], 1)

            pipelined(dve, message_prepare, message_step)

            with dve.Fori(0, NI) as i:
                for k in range(SETS):
                    one_hot(k, i, 3, msg, D)
            dve.wait_ge(s_agg, 3)
            link(dve.tensor_tensor(x[:, :, :], x[:, :, :], agg[:, :, 0:D], ALU.add))
            link(dve.tensor_tensor(x[:, :, :], x[:, :, :], l2b[:, :].unsqueeze(1).broadcast_to([BP, NB, D]), ALU.add))
            layernorm_relu()

            link(dve.tensor_scalar(gw2[:, :], gw2[:, :], 0.5, None, ALU.mult))
            link(dve.tensor_scalar(gb2[:, :], gb2[:, :], 0.5, None, ALU.mult))
            for k in range(SETS):
                dve.wait_ge(s_used[k], 1 + 4 * NI)
            link(dve.memset(gel[:, :, :, 0, D:D + 1].rearrange("p k j n -> p (k j) n"), 1.0))
            def split(parts, value, rest, step):
                step(dve.tensor_copy(parts(0), value))
                step(dve.tensor_tensor(rest, value, parts(0), ALU.subtract))
                step(dve.tensor_copy(parts(1), rest))
                return dve.tensor_tensor(parts(2), rest, parts(1), ALU.subtract)

            def edge_prepare(i, k):
                indices(k, i, 4, 3, 0)
                done = [0]

                def step(ins):
                    done[0] += 1
                    ins.then_inc(s_sp, 1)
                    dve.wait_ge(s_sp, (i * SETS + k) * 3 + done[0])

                split(lambda m: attr_parts[:, k, :, m, :], edges[:, k, :, 5:PW], attr_rest[:, k, :, :],
                      step).then_inc(s_atp[k], 1)

            def edge_step(i, k, last, _):
                dve.wait_ge(s_gel[k], i + 1)
                dve.tensor_tensor(gprod[:, :, :], gel[:, k, :, 1, 0:D],
                                  gw2[:, :].unsqueeze(1).broadcast_to([128, GT, D]), ALU.mult).then_inc(s_prod, 1)
                dve.wait_ge(s_prod, i * SETS + (k + 1))
                dve.tensor_reduce(gsum[:, k, :], gprod[:, :, :], AX_X, ALU.add).then_inc(s_dot[k], 1)
                if not isinstance(i, int) or k < 2:
                    edge_prepare(*following(*following(i, k)))
                dve.wait_ge(s_gate[k], i + 1)
                dve.tensor_scalar(gate[:, k, :], gsum[:, k, :], 0.5, 0.5, ALU.mult, ALU.add).then_inc(s_gst, 1)
                dve.wait_ge(s_gst, i * SETS + (k + 1))
                one_hot(k, i, 4, edges, 1, lambda j: gate[:, k, j:j + 1])

            after("tab3")
            tab3 = tab[:, :].rearrange("p (b f) -> p b f", f=2 * D)
            split(lambda m: tab_parts[:, :, m, :], tab3, tab3, link).then_inc(s_parts, 1)
            link(dve.tensor_copy(ident_b[:, :], ident[:, :]))
            we = wt[0:3 * DE, WI["mW1e"]:WI["mW1e"] + 2, :].rearrange("p w f -> p (w f)")
            link(split(lambda m: we_parts[:, m, :], we, we, link))
            dve.wait_ge(s_tab, 48)
            dve.sem_inc(s_norm, 1)
            edge_prepare(0, 0)
            pipelined(dve, lambda i, k: edge_prepare(0, 1), edge_step)

            dve.wait_ge(s_mm, FIRST["msgT"] + SIZE["msgT"])
            dve.memset(aT[D:D + 1, :], 1.0).then_inc(s_norm, 1)
            after("up")
            link(dve.tensor_tensor(z[:, :, :], z[:, :, :], h[:, :, :], ALU.add))
            centre(z[:, :, :])
            q = inverse_root(1.0 / D, 1e-5)
            link(dve.tensor_tensor(tmp[:, :, :], tmp[:, :, :], wide(q), ALU.mult))
            link(dve.tensor_tensor(tmp[:, :, :], tmp[:, :, :], ln_g[:, :].unsqueeze(1).broadcast_to([BP, NB, D]), ALU.mult))
            link(dve.tensor_tensor(tmp[:, :, :], tmp[:, :, :], ln_b[:, :].unsqueeze(1).broadcast_to([BP, NB, D]), ALU.add))
            dve.tensor_tensor(z[:, :, :], x[:, :, :], tmp[:, :, :], ALU.add).then_inc(s_res, 1)

        @block.scalar
        def _(act):
            roots = [0]

            def root():
                act.wait_ge(s_var, roots[0] + 1)
                act.activation(stat[:, 3, :], stat[:, 2, :], ACT.Sqrt).then_inc(s_sd, 1)
                roots[0] += 1

            def evacuate(step, dst, src, func=ACT.Copy):
                for j in range(SIZE[step]):
                    g = FIRST[step] + j
                    act.wait_ge(s_mm, g + 1)
                    act.activation(dst(j), src(j, psum[:, node_bank(g), :]), func).then_inc(s_ev, 1)

            def turned(to, rows=D):
                return (lambda j: to[0:rows, 4 * BP * j:min(4 * BP * (j + 1), N)],
                        lambda j, bank: bank[0:rows, 0:min(4 * BP, N - 4 * BP * j)])

            def blocks(to):
                return (lambda j: to[:, 5 * j:5 * j + 5, :].rearrange("p b f -> p (b f)"),
                        lambda j, bank: bank[0:BP, 0:5 * D])

            tab_b = tab[:, 0:NB * D].rearrange("p (b f) -> p b f", f=D)

            def aggregate(loop, n):
                for k in range(SETS):
                    act.wait_ge(s_used[k], 1 + (loop + 1) * NI)
                for j in range(5):
                    ins = act.activation(agg[:, 5 * j:5 * j + 5, :].rearrange("p b f -> p (b f)"),
                                         psum[0:BP, j, 0:5 * AW], ACT.Copy)
                ins.then_inc(s_agg, 1)

            root()
            evacuate("h0T", *turned(hT))
            evacuate("tab0", *blocks(tab_b))

            act.wait_ge(s_meta, 1)
            with act.Fori(0, NIS) as i:
                for k in range(SETS):
                    act.wait_ge(s_fr[k], i + 1)
                    act.activation(edges[0:EP, k, :, 0:5], meta[:, bass.ds(i * BODY + k * GT, GT), :],
                                   ACT.Copy).then_inc(s_ms[k], 1)

            evacuate("self0", *turned(sT))

            act.wait_ge(s_padm, 16 * NI)
            for k in range(SETS):
                act.sem_inc(s_exp[k], 1)
            def masked_weights(i, k):
                act.wait_ge(s_pen[k], i + 1)
                for j in range(GT):
                    ins = act.activation(val[:, k, j, :], pen[:, k, j, :], ACT.Identity, bias=edges[:, k, j, 2:3])
                ins.then_inc(s_val[k], 1)

            def tile_step(i, k, last, _):
                if not last:
                    masked_weights(*following(i, k))
                act.wait_ge(s_mx[k], i + 1)
                for j in range(GT):
                    at = psum[0:BP, 5 + k % 2, 128 * j:128 * j + 128]
                    ins = act.activation(at, at, ACT.Exp, bias=nmx[:, k, j:j + 1], accum_out=den[:, k, j:j + 1])
                ins.then_inc(s_exp[k], 1)
                act.wait_ge(s_exp[k], 2 * i + 2)
                act.activation(den_all[:, bass.ds(i * BODY + k * GT, GT)], den[:, k, :], ACT.Copy).then_inc(s_exp[k], 1)

            pipelined(act, masked_weights, tile_step)

            aggregate(0, 1)
            evacuate("agg0T", *turned(aT))
            evacuate("z0", *blocks(z))
            act.wait_ge(s_seg, 1)
            act.activation(nmx_full, nmx_full, ACT.Exp).then_inc(s_segx, 1)
            root()
            evacuate("h1T", *turned(hT))
            act.wait_ge(s_tab, 16)
            evacuate("tab1", *blocks(tab_b))
            evacuate("self1", *turned(sT))
            aggregate(1, 2)
            evacuate("agg1T", *turned(aT))
            evacuate("z1", *blocks(z))
            root()
            root()
            evacuate("h2T", *turned(hT))
            evacuate("y", *blocks(z), func=ACT.Relu)
            root()
            evacuate("h3T", *turned(hT))
            act.wait_ge(s_tab, 32)
            evacuate("sup", *blocks(tab_b))

            with act.Fori(0, NI) as i:
                for k in range(SETS):
                    act.wait_ge(s_ht[k], i + 1)
                    act.activation(hotT[:, k, :], psum[0:BP, 5 + k % 2, :], ACT.Copy).then_inc(s_hte[k], 1)

            aggregate(3, 3)
            root()
            evacuate("h4T", *turned(hT))
            evacuate("tab3",
                     lambda j: tab[:, 4 * D * j:min(4 * D * (j + 1), 2 * D * NB)],
                     lambda j, bank: bank[0:BP, 0:min(4 * D, 2 * D * (NB - 2 * j))])

            def turn_attr(i, k):
                act.wait_ge(s_attT[k], i + 1)
                act.activation(attrT[:, k, :], attr_bank, ACT.Copy).then_inc(s_atte[k], 1)

            def hidden(i, k):
                act.wait_ge(s_hid[k], i + 1)
                for half in range(2):
                    ins = act.activation(gel[:, k, 2 * half:2 * half + 2, :, 0:D],
                                         psum[:, 6 + half, 0:4 * D].rearrange("p (j s f) -> p j s f", j=2, s=2), ACT.Gelu)
                ins.then_inc(s_gel[k], 1)

            def edge_step(i, k, last, _):
                if not last:
                    turn_attr(*following(i, k))
                act.wait_ge(s_dot[k], i + 1)
                act.activation(gsum[:, k, :], gsum[:, k, :], ACT.Tanh, bias=gb2[:, 0:1]).then_inc(s_gate[k], 1)
                if not last:
                    hidden(*following(i, k))

            def edge_first(i, k):
                turn_attr(i, k)
                hidden(i, k)

            pipelined(act, edge_first, edge_step)

            aggregate(4, 4)
            evacuate("agg3T", *turned(aT, D + 1))
            evacuate("msgT", *turned(sT))
            act.wait_ge(s_norm, 3)
            evacuate("uT", *turned(aT), func=ACT.Gelu)
            evacuate("up", *blocks(z))
            root()

        @block.tensor
        def _(pe):
            def open_group(g):
                if g >= 3:
                    pe.wait_ge(s_ev, g - 2)
                return psum[:, node_bank(g), :]

            def chunk(j):
                return 4 * BP * j, min(4 * BP, N - 4 * BP * j)

            def transpose_blocks(step, src, rows=D):
                for j in range(SIZE[step]):
                    bank = open_group(FIRST[step] + j)
                    for q in range(min(4, NB - 4 * j)):
                        ins = pe.transpose(bank[0:rows, BP * q:BP * q + BP], src[:, 4 * j + q, 0:rows], ident[0:BP, 0:BP])
                    ins.then_inc(s_mm, 1)

            def to_nodes(step, terms):
                for j in range(SIZE[step]):
                    bank = open_group(FIRST[step] + j)
                    for q in range(5):
                        b = 5 * j + q
                        for m, (lhs, rows, w) in enumerate(terms):
                            ins = pe.matmul(bank[0:BP, D * q:D * q + D], lhs[0:rows, BP * b:BP * b + BP],
                                            wt[0:rows, WI[w], :], start=(m == 0), stop=(m == len(terms) - 1))
                    ins.then_inc(s_mm, 1)

            def to_features(step, terms):
                for j in range(SIZE[step]):
                    bank = open_group(FIRST[step] + j)
                    lo, n = chunk(j)
                    for m, (rhs, rows, w) in enumerate(terms):
                        ins = pe.matmul(bank[0:D, 0:n], wt[0:rows, WI[w], :], rhs[0:rows, lo:lo + n],
                                        start=(m == 0), stop=(m == len(terms) - 1))
                    ins.then_inc(s_mm, 1)

            def evacuated(step):
                pe.wait_ge(s_ev, FIRST[step] + SIZE[step])

            def zero_sums():
                for j in range(5):
                    pe.matmul(psum[0:BP, j, :], zrow[:, 0:BP], zrow[:, :], start=True, stop=True)

            def add_tile(k, j, cols, rhs):
                width = rhs.shape[-1]
                return pe.matmul(acc[:, bass.ds(cols[k * GT + j], width)], hot[:, k, j, :], rhs,
                                 start=False, stop=True, skip_group_check=True)

            def columns(tbl, top, i):
                return nc.values_load_multi_w_load_instructions(
                    tbl[0:1, bass.ds(i * BODY, BODY)], engines=(mybir.EngineType.PE,), min_val=0, max_val=top,
                    skip_runtime_bounds_check_because="the table holds the columns of blocks 0 to 24 only")[1]

            ACC_TOP = 4 * 512 + 4 * AW
            SUP_TOP = (NB - 1) * D

            pe.wait_ge(s_const, 1)
            pe.wait_ge(s_w, 16 * WEIGHT_LOADS)
            pe.wait_ge(s_h, 1)
            transpose_blocks("h0T", h)
            evacuated("h0T")
            to_nodes("tab0", [(hT, D + 1, "W0_0")])
            for n in range(2):
                pe.wait_ge(s_cnt, n + 1)
                pe.matmul(psum[0:EP, 0, 0:NB], upper[0:EP, 0:EP], count[:, :], start=True, stop=True)
                pe.matmul(psum[0:EP, 0, 32:32 + NB], ones[0:EP, 0:EP], count[:, :], start=True, stop=True).then_inc(s_pre, 1)

            for k in range(SETS):
                pe.wait_ge(s_sc[k], 16 * GT * NIS)
            to_features("self0", [(hT, D + 1, "W1_0")])

            for k in range(SETS):
                pe.sem_inc(s_used[k], 1)
            evacuated("self0")
            zero_sums()
            def turn_weights(i, k):
                pe.wait_ge(s_val[k], i + 1)
                pe.wait_ge(s_exp[(k + 2) % 4], 2 * i + (1 if k < 2 else 2))
                for j in range(GT):
                    ins = pe.transpose(psum[0:BP, 5 + k % 2, 128 * j:128 * j + 128], val[:, k, j, :], ident[:, :])
                ins.then_inc(s_vt[k], 1)

            def tile_step(i, k, last, cols):
                if not last:
                    turn_weights(*following(i, k))
                pe.wait_ge(s_hot[k], i + 1)
                pe.wait_ge(s_g[k], (i + 1) * (16 * GT))
                for j in range(GT):
                    ins = add_tile(k, j, cols, gat[:, k, j, 0:D])
                ins.then_inc(s_used[k], 1)

            pipelined(pe, turn_weights, tile_step, lambda i: columns(acc_d, ACC_TOP, i))
            pe.wait_ge(s_agg, 1)
            for k in range(SETS):
                pe.wait_ge(s_exp[k], 2 * NI + 1)
            transpose_blocks("agg0T", agg)
            evacuated("agg0T")
            pe.wait_ge(s_norm, 1)
            to_nodes("z0", [(sT, D + 1, "W2a_0"), (aT, D, "W2b_0")])
            pe.wait_ge(s_h, 2)
            transpose_blocks("h1T", h)
            evacuated("h1T")
            to_nodes("tab1", [(hT, D + 1, "W0_1")])
            to_features("self1", [(hT, D + 1, "W1_1")])

            evacuated("self1")
            zero_sums()
            with pe.Fori(0, NI) as i:
                cols = columns(acc_d, ACC_TOP, i)
                for k in range(SETS):
                    pe.wait_ge(s_hot[k], i + (1 + NI))
                    pe.wait_ge(s_g[k], (i + (1 + NI)) * (16 * GT))
                    for j in range(GT):
                        ins = add_tile(k, j, cols, gat[:, k, j, 0:D])
                    ins.then_inc(s_used[k], 1)
            pe.wait_ge(s_agg, 2)
            transpose_blocks("agg1T", agg)
            evacuated("agg1T")
            to_nodes("z1", [(sT, D + 1, "W2a_1"), (aT, D, "W2b_1")])

            pe.wait_ge(s_h, 3)
            transpose_blocks("h2T", h)
            evacuated("h2T")
            to_nodes("y", [(hT, D + 1, "Wv")])

            pe.wait_ge(s_h, 4)
            transpose_blocks("h3T", h)
            evacuated("h3T")
            to_nodes("sup", [(hT, D, "Wl2")])
            evacuated("sup")
            def turn_hot(i, k):
                pe.wait_ge(s_hot[k], i + (1 + 2 * NI))
                for j in range(GT):
                    ins = pe.transpose(psum[0:BP, 5 + k % 2, 128 * j:128 * j + 128], hot[:, k, j, :], ident[:, :])
                ins.then_inc(s_ht[k], 1)

            def message_step(i, k, last, cols):
                if not last:
                    turn_hot(*following(i, k))
                pe.wait_ge(s_hte[k], i + 1)
                for j in range(GT):
                    ins = pe.matmul(psum[:, k, D * j:D * j + D], hotT[:, k, 128 * j:128 * j + 128],
                                    tab[:, bass.ds(cols[k * GT + j], D)], start=True, stop=True)
                ins.then_inc(s_sup[k], 1)

            pipelined(pe, turn_hot, message_step, lambda i: columns(sup_d, SUP_TOP, i))
            for k in range(SETS):
                pe.wait_ge(s_msg[k], NI)
            zero_sums()
            with pe.Fori(0, NI) as i:
                cols = columns(acc_s, ACC_TOP, i)
                for k in range(SETS):
                    pe.wait_ge(s_hot[k], i + (1 + 3 * NI))
                    pe.wait_ge(s_ed[k], (i + (1 + 3 * NI)) * 16)
                    for j in range(GT):
                        ins = add_tile(k, j, cols, msg[:, k, j, 0:D])
                    ins.then_inc(s_used[k], 1)

            pe.wait_ge(s_h, 5)
            transpose_blocks("h4T", h)
            evacuated("h4T")
            for j in range(SIZE["tab3"]):
                bank = open_group(FIRST["tab3"] + j)
                for q in range(min(2, NB - 2 * j)):
                    b = 2 * j + q
                    for half, w in enumerate(("mW1x", "gW1x")):
                        ins = pe.matmul(bank[0:BP, D * (2 * q + half):D * (2 * q + half) + D], hT[0:D + 1, BP * b:BP * b + BP],
                                        wt[0:D + 1, WI[w], :], start=True, stop=True)
                ins.then_inc(s_mm, 1)
            evacuated("tab3")
            zero_sums()
            def edge_part(i, k):
                pe.wait_ge(s_atp[k], i + 1)
                for j in range(GT):
                    ins = pe.transpose(attr_bank[:, 128 * j:128 * j + 128],
                                       attr_parts[:, k, j, :, :].rearrange("p s f -> p (s f)"), ident_b[:, :])
                ins.then_inc(s_attT[k], 1)
                pe.wait_ge(s_atte[k], i + 1)
                if k:
                    pe.wait_ge(s_gel[k - 1], i + 1)
                elif not isinstance(i, int):
                    pe.wait_ge(s_gel[SETS - 1], i)
                for j in range(GT):
                    to = psum[:, 6 + j // 2, 2 * D * (j % 2):2 * D * (j % 2) + 2 * D]
                    for m in range(3):
                        pe.matmul(to, attrT[:, k, 128 * j:128 * j + 128], we_parts[:, m, :], start=(m == 0), stop=False)
                    if j == 0:
                        pe.wait_ge(s_g[k], (i + (1 + 2 * NI)) * (16 * GT))
                    for m in range(3):
                        ins = pe.matmul(to, ident_b[:, :], gat3[:, k, j, 2 * D * m:2 * D * m + 2 * D], start=False, stop=(m == 2))
                ins.then_inc(s_hid[k], 1)

            def edge_step(i, k, last, cols):
                if not last:
                    edge_part(*following(i, k))
                pe.wait_ge(s_hot[k], i + (1 + 4 * NI))
                for j in range(GT):
                    ins = add_tile(k, j, cols, gel[:, k, j, 0, :])
                ins.then_inc(s_used[k], 1)

            pe.wait_ge(s_norm, 2)
            pipelined(pe, edge_part, edge_step, lambda i: columns(acc_d, ACC_TOP, i))
            pe.wait_ge(s_agg, 4)
            transpose_blocks("agg3T", agg, D + 1)
            evacuated("agg3T")
            to_features("msgT", [(aT, D + 1, "mW2")])
            evacuated("msgT")
            to_features("uT", [(hT, D + 1, "uW1a"), (sT, D, "uW1b")])
            evacuated("uT")
            to_nodes("up", [(aT, D + 1, "uW2")])


_INS = ["x", "src", "dst", "edge_attr_32", "edge_weight", "L0_gnn_W0", "L0_gnn_b0", "L0_gnn_W1", "L0_gnn_b1",
        "L0_gnn_W2", "L0_gnn_b2", "L1_gnn_Wv", "L1_gnn_bv", "L2_gnn_weight", "L2_gnn_b",
        "L3_gnn_mW1", "L3_gnn_mb1", "L3_gnn_mW2", "L3_gnn_mb2", "L3_gnn_gW1", "L3_gnn_gb1", "L3_gnn_gW2",
        "L3_gnn_gb2", "L3_gnn_uW1", "L3_gnn_ub1", "L3_gnn_uW2", "L3_gnn_ub2", "L3_gnn_ln_g", "L3_gnn_ln_b"]


def kernel(**inputs):
    import numpy as _np
    import concourse.bacc as _bacc
    from concourse import mybir as _mybir
    from concourse.bass_utils import run_bass_kernel_spmd as _run

    nc = _bacc.Bacc("TRN2", target_bir_lowering=False, num_devices=1)
    arrays, aps = {}, {}
    for name in _INS:
        v = _np.ascontiguousarray(inputs[name])
        arrays[f"in_{name}_dram"] = v
        aps[name] = nc.dram_tensor(f"in_{name}_dram", v.shape, _mybir.dt.from_np(v.dtype), kind="ExternalInput").ap()
    out = nc.dram_tensor("out_0_dram", (N, D), _mybir.dt.float32, kind="ExternalOutput").ap()
    build(nc, aps, out)
    r = _run(nc, [arrays], core_ids=[0])
    return r.results[0]["out_0_dram"]
```

```python
from contextlib import ExitStack

import concourse.bass as bass
from concourse import mybir

ALU = mybir.AluOpType
ACT = mybir.ActivationFunctionType
AX_X = mybir.AxisListType.X
F32 = mybir.dt.float32
I32 = mybir.dt.int32
BF16 = mybir.dt.bfloat16

D = 96
DE = 32
NB = 25
BP = 125
N = NB * BP
EP, EC = 125, 800
E = EP * EC
T = 816
SETS, GT = 4, 4
BODY = SETS * GT
NI = T // BODY
NIS = EC // BODY
META = 5
PW = META + DE
MW = D + 1
AW = D + 1
PER_BANK = 5
ROWS = 128 * T
EVEN = BP // 16 * 16
SPREAD = 32
BIG = 1e38
assert N == 3125 and E == 100000 and T * 128 >= E + 127 * NB and PER_BANK * AW <= 512

WEIGHTS = ["W0_0", "W0_1", "W1_0", "W1_1", "W2a_0", "W2a_1", "W2b_0", "W2b_1", "Wv", "Wl2",
           "mW1x", "gW1x", "mW1e", "gW1e", "mW2", "uW1a", "uW1b", "uW2"]
DVE_COUNTS = (14, 12)
HALF_T = T // 2
assert NI == 2 * NB + 1
WEIGHT_LOADS = 39
WI = {n: i for i, n in enumerate(WEIGHTS)}

NODE_STEPS = [("h0T", 7), ("tab0", 5), ("self0", 7), ("agg0T", 7), ("z0", 5),
              ("h1T", 7), ("tab1", 5), ("self1", 7), ("agg1T", 7), ("z1", 5),
              ("h2T", 7), ("y", 5), ("h3T", 7), ("sup", 5),
              ("h4T", 7), ("tab3", 13), ("agg3T", 7), ("msgT", 7), ("uT", 7), ("up", 5)]
FIRST, SIZE = {}, {}
_n = 0
for _name, _k in NODE_STEPS:
    FIRST[_name], SIZE[_name] = _n, _k
    _n += _k


def following(i, k):
    return (i, k + 1) if k < SETS - 1 else (i + 1, 0)


def ahead(i, k, m):
    if k + m < SETS:
        return i, k + m
    return None if isinstance(i, int) and i == NI - 1 else (i + 1, k + m - SETS)


def pipelined(eng, first, step):
    first(0, 0)
    with eng.Fori(0, NI - 1) as i:
        for k in range(SETS):
            step(i, k, False)
    for k in range(SETS):
        step(NI - 1, k, k == SETS - 1)


def pieces_for(j):
    return -(-min(4 * j + 4, NB) // PER_BANK)


def spread(eng, dst, src, done):
    n = dst.shape[0]
    for rows in (slice(0, EVEN), slice(EVEN, n)):
        eng.dma_start(dst[rows], src[rows]).then_inc(done, 16)


def node_bank(g):
    return 5 + g % 3


def build(nc, a, out):
    ctx = ExitStack()
    with ctx:
        def sb(name, shape, dt=F32):
            return ctx.enter_context(nc.sbuf_tensor(name, shape, dt))

        def sem(name):
            return ctx.enter_context(nc.semaphore(name))

        payload = nc.dram_tensor("payload", (128, T * PW), F32, kind="Internal").ap()
        messages = nc.dram_tensor("messages", (128, T * MW), F32, kind="Internal").ap()
        meta_sorted = nc.dram_tensor("meta_sorted", (E + 128, META), F32, kind="Internal").ap()
        attr_sorted = nc.dram_tensor("attr_sorted", (E + 128, DE), F32, kind="Internal").ap()
        payload_rows = payload.rearrange("p (t w) -> (p t) w", w=PW)
        message_rows = messages.rearrange("p (t w) -> (p t) w", w=MW)
        table = [nc.dram_tensor(f"table{d}", (N, D), F32, kind="Internal").ap() for d in range(2)]
        table3 = nc.dram_tensor("table3", (N, 3 * 2 * D), BF16, kind="Internal").ap()

        x = sb("x", [BP, NB, D])
        h = sb("h", [BP, NB, D])
        z = sb("z", [BP, NB, D])
        tmp = sb("tmp", [BP, NB, D])
        agg = sb("agg", [BP, NB, AW])
        tab = sb("tab", [BP, NB * 2 * D])
        hT = sb("hT", [D + 1, N])
        wt = sb("wt", [D + 1, len(WEIGHTS), D])
        region = sb("region", [128, 11600])
        meta = region[0:EP, 0:EC * META].rearrange("p (c w) -> p c w", w=META)

        def sort_array(i):
            return region[0:EP, (META + i) * EC:(META + i + 1) * EC]

        key_d, blk_d, blk_s, pos, mask, csum, prod, ones_row, place = (sort_array(i) for i in range(9))
        behind = tmp[0:NB, :, :].rearrange("p b f -> p (b f)")[:, 0:T]
        start_row = tmp[0:1, :, :].rearrange("p b f -> p (b f)")[:, T:2 * T]
        two_masks = z[:, :, :].rearrange("p b f -> p (b f)")[:, 0:2 * EC].rearrange("p (a c) -> p a c", a=2)
        sT = region[0:D + 1, 0:N]
        aT = region[0:D + 1, N:2 * N]
        nmx_all = region[0:BP, 2 * N:2 * N + T]
        den_all = region[0:BP, 2 * N + T:2 * N + 2 * T]
        blk_t = sb("blk_t", [128, T])
        seg_tmp = region[0:BP, 2 * N + 2 * T:2 * N + 3 * T]
        nmx_full = region[0:BP, 2 * N + 3 * T:2 * N + 4 * T]
        place_slot = sb("place_slot", [EP, SETS, GT], I32)
        acc_d = sb("acc_d", [1, T], I32)
        acc_s = sb("acc_s", [1, T], I32)
        sup_d = sb("sup_d", [1, T], I32)
        iota_i = sb("iota_i", [128, 128], I32)
        iota = sb("iota", [128, 128])
        part = sb("part", [128, 1])
        part_step = sb("part_step", [128, 1])
        iota_t = sb("iota_t", [BP, T])
        ident = sb("ident", [128, 128])
        upper = sb("upper", [128, 128])
        ones = sb("ones", [128, 128])
        zrow = sb("zrow", [1, 512])
        minus_b = sb("minus_b", [EP, NB])
        count = sb("count", [EP, 2, NB + 1])
        base = sb("base", [EP, 2, NB])
        waste = sb("waste", [EP, NB])
        bucket_col = sb("bucket_col", [NB, 3])
        start_d = sb("start_d", [1, T], I32)
        unsorted = sb("unsorted", [1, 1], I32)
        need = sb("need", [EP, NB])
        need_i = sb("need_i", [EP, NB], I32)
        ends = sb("ends", [EP, 2, NB])
        node_d = sb("node_d", [128, SETS, GT])
        node_all = sb("node_all", [128, T])
        index_all = region[:, 10770:10770 + T].bitcast(I32)
        row_s = sb("row_s", [128, SETS, GT])
        stat = sb("stat", [BP, 8, NB])
        seg_m = sb("seg_m", [BP, NB])
        seg_d = sb("seg_d", [BP, NB])
        share = sb("share", [BP, NB])
        l2b = sb("l2b", [BP, D])
        ln_g = sb("ln_g", [BP, D])
        ln_b = sb("ln_b", [BP, D])
        gw2 = sb("gw2", [128, D])
        gb2 = sb("gb2", [128, 1])
        edges = sb("edges", [128, SETS, GT, PW])
        index = sb("index", [128, SETS, GT], I32)
        gat = sb("gat", [128, SETS, GT, 3 * D])
        pad_pay = gat[:, :, :, :].rearrange("p k j f -> p (k j f)")[:, 0:16 * PW].rearrange("p (t w) -> p t w", w=PW)
        gat3 = gat[:, :, :, :].bitcast(BF16)
        hot = sb("hot", [128, SETS, GT, BP])
        work = sb("work", [128, 4096])
        pen = work[:, 0:2000].rearrange("p (k j n) -> p k j n", k=SETS, j=GT)
        val = work[:, 2048:4048].rearrange("p (k j n) -> p k j n", k=SETS, j=GT)
        hotT = work[0:BP, 0:2048].rearrange("p (k e) -> p k e", k=SETS)
        pad_msg = work[:, 2048:2048 + 16 * MW].rearrange("p (t w) -> p t w", w=MW)
        msg = work[:, 2048:2048 + BODY * MW].rearrange("p (k j n) -> p k j n", k=SETS, j=GT)
        gel = work[:, 0:BODY * 2 * (D + 1)].rearrange("p (k j s n) -> p k j s n", k=SETS, j=GT, s=2)
        nmx = sb("nmx", [BP, SETS, GT])
        den = sb("den", [BP, SETS, GT])
        tab_parts = region[0:BP, 0:NB * 3 * D].bitcast(BF16).rearrange("p (b s f) -> p b s f", b=NB, s=3)
        attrT = region[0:3 * DE, 0:SETS * GT * 64].bitcast(BF16).rearrange("p (k e) -> p k e", k=SETS)
        attr_rest = region[:, 8800:8800 + BODY * DE].rearrange("p (k j f) -> p k j f", k=SETS, j=GT)
        attr_parts = region[:, 9400:9400 + BODY * 3 * DE // 2].bitcast(BF16).rearrange(
            "p (k j s f) -> p k j s f", k=SETS, j=GT, s=3)
        we_parts = sb("we_parts", [3 * DE, 3, 2 * D], BF16)
        ident_b = sb("ident_b", [128, 128], BF16)
        gprod = region[:, 8400:8400 + GT * D].rearrange("p (j f) -> p j f", j=GT)
        gsum = sb("gsum", [128, SETS, GT])
        gate = sb("gate", [128, SETS, GT])
        psum = ctx.enter_context(nc.psum_tensor("psum", [128, 8, 512], F32))
        attr_bank = psum[0:3 * DE, 5, 0:GT * 64].bitcast(BF16)
        acc = psum[0:BP, 0:5, :].rearrange("p a b -> p (a b)")

        s_w = sem("weights_loaded")
        s_x = sem("x_loaded")
        s_key = sem("keys_loaded")
        s_iota = sem("iotas_made")
        s_const = sem("constants_made")
        s_pad = sem("pad_tiles_made")
        s_padw = sem("payload_pads_written")
        s_padm = sem("message_pads_written")
        s_vl = sem("vector_link")
        s_al = sem("scalar_link")
        s_var = sem("variance_ready")
        s_sd = sem("sqrt_ready")
        s_h = sem("h_ready")
        s_mm = sem("node_group_done")
        s_ev = sem("node_group_evacuated")
        s_tab = sem("table_stored")
        s_cnt = sem("bucket_counts_ready")
        s_pre = sem("bucket_prefix_ready")
        s_blk = sem("buckets_ready")
        s_mask = sem("src_mask_ready")
        s_mfre = sem("src_mask_used")
        s_flag = sem("order_known")
        s_tg = sem("tile_step_ready")
        s_tp = sem("tile_product_done")
        s_gl = sem("general_link")
        s_copy = sem("features_copied")
        s_stage = sem("sorted_rows_stored")
        s_rows = sem("edge_rows_in_dram")
        s_cact = sem("counts_by_scalar")
        s_sg = sem("segment_steps")
        s_meta = sem("meta_ready")
        s_agg = sem("agg_evacuated")
        s_norm = sem("node_update_done")
        s_seg = sem("segment_exponent_ready")
        s_segx = sem("segment_exp_done")
        s_out = sem("out_stored")
        s_res = sem("result_ready")
        s_parts = sem("table3_parts_ready")
        s_sp = sem("attr_split_steps")

        def sems(name):
            return [sem(f"{name}{k}") for k in range(SETS)]

        s_fr = sems("slot_free")
        s_at = sems("attr_loaded")
        s_ms = sems("meta_in_slot")
        s_edf = sems("edges_slot_free")
        s_sc = sems("payload_scattered")
        s_ed = sems("edges_loaded")
        s_fe = sems("features_loaded")
        s_ml = sems("messages_loaded")
        s_loc = sem("node_in_block_ready")
        s_row = sem("row_steps")
        s_keep = sem("tiles_kept")
        s_ix = sems("index_ready")
        s_g = sems("rows_gathered")
        s_hot = sems("hot_ready")
        s_used = sems("group_used")
        s_pen = sems("penalty_ready")
        s_val = sems("masked_weights_ready")
        s_vt = sems("masked_weights_transposed")
        s_mx = sems("tile_max_ready")
        s_exp = sems("tile_exp_done")
        s_hte = sems("hotT_evacuated")
        s_sup = sems("support_rows_ready")
        s_msg = sems("messages_ready")
        s_msc = sems("messages_scattered")
        s_mfree = sems("message_slot_free")
        s_attT = sems("attr_transposed")
        s_atte = sems("attrT_evacuated")
        s_atp = sems("attr_parts_ready")
        s_hid = sems("edge_hidden_ready")
        s_gel = sems("gelu_done")
        s_dot = sems("gate_dot_ready")
        s_gate = sem("tanh_ready")
        s_prod = sem("gate_products_ready")
        s_gst = sem("gate_steps")

        def dst_order(eng):
            return eng.value_load(unsorted[0:1, 0:1], min_val=0, max_val=EP)

        block = ctx.enter_context(nc.Block())

        @block.sync
        def _(sp):
            def row(v):
                return v.rearrange("(o n) -> o n", o=1)

            spread(sp, key_d.bitcast(I32), a["dst"].rearrange("(p c) -> p c", p=EP), s_key)
            spread(sp, csum.bitcast(I32), a["src"].rearrange("(p c) -> p c", p=EP), s_key)
            spread(sp, prod, a["edge_weight"].rearrange("(p c) -> p c", p=EP), s_key)
            nxt = pos.bitcast(I32)
            spread(sp, nxt[0:EP - 1, :], a["dst"][1:1 + (EP - 1) * EC].rearrange("(p c) -> p c", c=EC), s_key)
            sp.dma_start(nxt[EP - 1:EP, 0:EC - 1], row(a["dst"][1 + (EP - 1) * EC:E])).then_inc(s_key, 16)
            sp.dma_start(nxt[EP - 1:EP, EC - 1:EC], row(a["dst"][E - 1:E])).then_inc(s_key, 16)
            spread(sp, x[:, :, :], a["x"].rearrange("(b p) f -> p b f", p=BP), s_x)

            def weight(name, w, b=None):
                sp.dma_start(wt[0:w.shape[0], WI[name], :], w).then_inc(s_w, 16)
                if b is not None:
                    sp.dma_start(wt[D:D + 1, WI[name], :], row(b)).then_inc(s_w, 16)

            for d in range(2):
                weight(f"W0_{d}", a["L0_gnn_W0"][d], a["L0_gnn_b0"][d])
                weight(f"W1_{d}", a["L0_gnn_W1"][d], a["L0_gnn_b1"][d])
                weight(f"W2a_{d}", a["L0_gnn_W2"][d, 0:D], a["L0_gnn_b2"][d])
                weight(f"W2b_{d}", a["L0_gnn_W2"][d, D:2 * D])
            weight("Wv", a["L1_gnn_Wv"], a["L1_gnn_bv"])
            weight("Wl2", a["L2_gnn_weight"])
            weight("mW1x", a["L3_gnn_mW1"][0:D], a["L3_gnn_mb1"])
            weight("gW1x", a["L3_gnn_gW1"][0:D], a["L3_gnn_gb1"])
            for part in range(3):
                at = slice(DE * part, DE * part + DE)
                sp.dma_start(wt[at, WI["mW1e"], :], a["L3_gnn_mW1"][D:D + DE]).then_inc(s_w, 16)
                sp.dma_start(wt[at, WI["gW1e"], :], a["L3_gnn_gW1"][D:D + DE]).then_inc(s_w, 16)
            weight("mW2", a["L3_gnn_mW2"], a["L3_gnn_mb2"])
            weight("uW1a", a["L3_gnn_uW1"][0:D], a["L3_gnn_ub1"])
            weight("uW1b", a["L3_gnn_uW1"][D:2 * D])
            weight("uW2", a["L3_gnn_uW2"], a["L3_gnn_ub2"])
            for dst, v in ((l2b, "L2_gnn_b"), (ln_g, "L3_gnn_ln_g"), (ln_b, "L3_gnn_ln_b")):
                sp.dma_start(dst[:, :], a[v].partition_broadcast(BP)).then_inc(s_w, 16)
            sp.dma_start(gw2[:, :], a["L3_gnn_gW2"].rearrange("n o -> (n o)").partition_broadcast(128)).then_inc(s_w, 16)
            sp.dma_start(gb2[:, :], a["L3_gnn_gb2"].partition_broadcast(128)).then_inc(s_w, 16)

            sp.wait_ge(s_pad, 2)
            pad_pay_flat = pad_pay[:, :, :].rearrange("p t w -> p (t w)")
            pad_msg_flat = pad_msg[:, :, :].rearrange("p t w -> p (t w)")
            with sp.Fori(0, NI) as i:
                sp.dma_start(messages[:, bass.ds(i * 16 * MW, 16 * MW)], pad_msg_flat).then_inc(s_padm, 16)

            sp.dma_start(attr_sorted[E:E + 128, :], pad_pay[:, 0, META:PW]).then_inc(s_copy, 16)

            tab96 = tab[:, 0:NB * D].rearrange("p (b f) -> p b f", f=D)
            sp.wait_ge(s_ev, FIRST["tab0"] + SIZE["tab0"])
            spread(sp, table[0].rearrange("(b p) f -> p b f", p=BP), tab96, s_tab)

            attr = a["edge_attr_32"].rearrange("(p c) f -> p c f", p=EP)

            def load_attr(i, k):
                sp.sem_inc(s_fr[k], 1)
                sp.dma_start(edges[0:EP, k, :, META:PW], attr[:, bass.ds(i * BODY + k * GT, GT), :]).then_inc(s_at[k], 16)

            sp.wait_ge(s_flag, 1)
            is_unsorted = dst_order(sp) > 0
            with sp.If(is_unsorted):
                with sp.Fori(0, NI) as i:
                    sp.dma_start(payload[:, bass.ds(i * 16 * PW, 16 * PW)], pad_pay_flat).then_inc(s_padw, 16)
                for k in range(SETS):
                    load_attr(0, k)
                with sp.Fori(1, NIS) as i:
                    for k in range(SETS):
                        sp.wait_ge(s_sc[k], i * (16 * GT))
                        load_attr(i, k)
                for k in range(SETS):
                    sp.wait_ge(s_sc[k], 16 * GT * NIS)
            with sp.Else():
                sp.wait_ge(s_meta, 1)
                spread(sp, meta_sorted[0:E, :].rearrange("(p c) w -> p (c w)", p=EP), region[0:EP, 0:EC * META], s_stage)
                sp.dma_start(meta_sorted[E:E + 128, :], pad_pay[:, 0, 0:META]).then_inc(s_stage, 16)
                sp.wait_ge(s_stage, SPREAD + 16)
            sp.wait_ge(s_copy, 16)
            sp.sem_inc(s_rows, 1)

            payload_tiles = payload.rearrange("p (t w) -> p t w", w=PW)

            def load_group(i, k, features, starts=None):
                for j in range(GT):
                    if starts is None:
                        tile = payload_tiles[:, bass.ds(i * BODY + k * GT + j, 1), :].rearrange("p t w -> p (t w)")
                        words, attrs = tile[:, 0:META], tile[:, META:PW]
                    else:
                        run = bass.ds(starts[k * GT + j], 128)
                        words, attrs = meta_sorted[run, :], attr_sorted[run, :]
                    if features:
                        sp.dma_start(edges[:, k, j, META:PW], attrs).then_inc(s_fe[k], 16)
                    else:
                        sp.dma_start(edges[:, k, j, 0:META], words).then_inc(s_ed[k], 16)

            def run_starts(i):
                return nc.values_load_multi_w_load_instructions(
                    start_d[0:1, bass.ds(i * BODY, BODY)], engines=(mybir.EngineType.SP,), min_val=0, max_val=E,
                    skip_runtime_bounds_check_because="the starts are cut off at E")[1]

            def load_edges(free, features=False):
                with sp.If(dst_order(sp) > 0):
                    with sp.Fori(0, NI) as i:
                        for k in range(SETS):
                            free(i, k)
                            load_group(i, k, features)
                with sp.Else():
                    with sp.Fori(0, NI) as i:
                        starts = run_starts(i)
                        for k in range(SETS):
                            free(i, k)
                            load_group(i, k, features, starts)

            def used(i, k):
                sp.wait_ge(s_used[k], i + 1)

            def read(nth):
                return lambda i, k: sp.wait_ge(s_edf[k], i + (1 + nth * NI))

            load_edges(used)
            sp.wait_ge(s_ev, FIRST["tab1"] + SIZE["tab1"])
            spread(sp, table[1].rearrange("(b p) f -> p b f", p=BP), tab96, s_tab)
            for k in range(SETS):
                sp.wait_ge(s_used[k], 1 + NI)
                sp.sem_inc(s_edf[k], 1)

            load_edges(read(0))
            for k in range(SETS):
                sp.wait_ge(s_msc[k], 16 * GT * NI)
            with sp.Fori(0, NI) as i:
                for k in range(SETS):
                    sp.wait_ge(s_used[k], i + (1 + 3 * NI))
                    sp.dma_start(msg[:, k, :, :].rearrange("p j w -> p (j w)"),
                                 messages[:, bass.ds((i * BODY + k * GT) * MW, GT * MW)]).then_inc(s_ml[k], 16)
            for c in range(NB // PER_BANK):
                blocks = slice(PER_BANK * c, PER_BANK * (c + 1))
                sp.wait_ge(s_parts, c + 1)
                spread(sp, table3.rearrange("(b p) f -> p b f", p=BP)[:, blocks, :],
                       tab_parts[:, blocks, :, :].rearrange("p b s f -> p b (s f)"), s_tab)
            sp.wait_ge(s_copy, 16 * (NB + 1))
            load_edges(read(1), features=True)
            for c in range(NB // PER_BANK):
                blocks = slice(PER_BANK * c, PER_BANK * (c + 1))
                sp.wait_ge(s_res, c + 1)
                spread(sp, out.rearrange("(b p) f -> p b f", p=BP)[:, blocks, :], z[:, blocks, :], s_out)
            sp.wait_ge(s_out, SPREAD * (NB // PER_BANK))

        @block.gpsimd
        def _(pool):
            pool.iota(iota_i[:, :], pattern=[[1, 128]], base=0, channel_multiplier=0).then_inc(s_iota, 1)
            pool.iota(part[:, :], pattern=[[0, 1]], base=0, channel_multiplier=1,
                      allow_small_or_imprecise_dtypes=True).then_inc(s_iota, 1)
            pool.iota(iota_t[:, :], pattern=[[1, T]], base=0, channel_multiplier=0,
                      allow_small_or_imprecise_dtypes=True).then_inc(s_iota, 1)

            def held(s, v):
                pool.wait_ge(s, v)
                pool.nop(nofuse=True)

            pool.wait_ge(s_cact, 2)
            for b in range(NB):
                if b >= 2:
                    pool.wait_ge(s_mfre, b - 1)
                pool.tensor_scalar(two_masks[:, b % 2, :], blk_s, float(b), None, ALU.is_equal).then_inc(s_mask, 1)

            pool.wait_ge(s_flag, 1)
            with pool.If(dst_order(pool) > 0):
                held(s_padw, 16 * NI)
                with pool.Fori(0, NIS) as i:
                    for k in range(SETS):
                        held(s_at[k], (i + 1) * 16)
                        held(s_ms[k], i + 1)
                        for j in range(GT):
                            pool.indirect_dma_start(
                                payload_rows, bass.IndirectOffsetOnAxis(ap=place_slot[:, k, j:j + 1], axis=0),
                                edges[0:EP, k, j, :], None).then_inc(s_sc[k], 16)

            def gather(nth_index, stored, tbl, dst):
                held(s_tab, SPREAD * stored)
                with pool.Fori(0, NI) as i:
                    for k in range(SETS):
                        held(s_ix[k], i + (1 + nth_index * NI))
                        for j in range(GT):
                            pool.indirect_dma_start(
                                dst(k, j), None, tbl,
                                bass.IndirectOffsetOnAxis(ap=index[:, k, j:j + 1], axis=0)).then_inc(s_g[k], 16)

            gather(0, 1, table[0], lambda k, j: gat[:, k, j, 0:D])
            gather(1, 2, table[1], lambda k, j: gat[:, k, j, 0:D])
            held(s_padm, 16 * NI)
            with pool.Fori(0, NI) as i:
                for k in range(SETS):
                    held(s_ix[k], i + (1 + 2 * NI))
                    held(s_msg[k], i + 1)
                    for j in range(GT):
                        pool.indirect_dma_start(
                            message_rows, bass.IndirectOffsetOnAxis(ap=index[:, k, j:j + 1], axis=0),
                            msg[:, k, j, :], None, bounds_check=ROWS - 1, oob_is_err=False).then_inc(s_msc[k], 16)
            gather(3, 2 + NB // PER_BANK, table3, lambda k, j: gat3[:, k, j, :])

        @block.vector
        def _(dve):
            links = [0]

            def link(ins):
                links[0] += 1
                ins.then_inc(s_vl, 1)
                dve.wait_ge(s_vl, links[0])

            def wide(s):
                return s.unsqueeze(2).broadcast_to([BP, s.shape[-1], D])

            dve.wait_ge(s_iota, 3)
            link(dve.tensor_copy(iota[:, :], iota_i[:, :]))
            link(dve.tensor_scalar(ident[:, :], iota[:, :], part[:, 0:1], None, ALU.is_equal))
            link(dve.tensor_scalar(upper[:, :], iota[:, :], part[:, 0:1], None, ALU.is_gt))
            link(dve.tensor_scalar(minus_b[:, :], iota[0:EP, 0:NB], -1.0, None, ALU.mult))
            link(dve.memset(ones[:, :], 1.0))
            link(dve.memset(bucket_col[:, 2:3], float(AW)))
            for m in range(1, NB // PER_BANK):
                link(dve.tensor_scalar(part_step[0:NB, :], part[0:NB, :], float(m * PER_BANK - 1),
                                       float(512 - PER_BANK * AW), ALU.is_equal, ALU.mult))
                link(dve.tensor_tensor(bucket_col[:, 2:3], bucket_col[:, 2:3], part_step[0:NB, :], ALU.add))
            link(dve.memset(zrow[:, :], 0.0))
            dve.memset(hT[D:D + 1, :], 1.0).then_inc(s_const, 1)
            link(dve.memset(pad_pay[:, :, :], 0.0))
            link(dve.memset(pad_msg[:, :, :], 0.0))
            link(dve.memset(pad_pay[:, :, 1:2], -1.0))
            link(dve.memset(pad_pay[:, :, 3:4], float(ROWS)))
            link(dve.memset(pad_pay[:, :, 4:5], -1.0))
            dve.memset(pad_msg[:, :, D:D + 1], -1.0).then_inc(s_pad, 2)

            roots = [0]

            def inverse_root(scale, eps):
                v, s0, r, q = stat[:, 2, :], stat[:, 3, :], stat[:, 4, :], stat[:, 5, :]
                roots[0] += 1
                dve.tensor_scalar(v, v, scale, eps, ALU.mult, ALU.add).then_inc(s_var, 1)
                dve.wait_ge(s_sd, roots[0])
                dve.wait_ge(s_var, roots[0])
                link(dve.reciprocal(r, s0))
                link(dve.tensor_tensor(q, v, r, ALU.mult))
                link(dve.tensor_tensor(q, q, s0, ALU.add))
                link(dve.tensor_scalar(r, q, 0.5, None, ALU.mult))
                link(dve.reciprocal(q, r))
                return q

            every = slice(0, NB)
            pieces = [slice(PER_BANK * c, PER_BANK * (c + 1)) for c in range(NB // PER_BANK)]

            def centre(v, c):
                link(dve.tensor_reduce(stat[:, 0, c], v[:, c, :], AX_X, ALU.add))
                link(dve.tensor_scalar(stat[:, 1, c], stat[:, 0, c], 1.0 / D, None, ALU.mult))
                link(dve.tensor_tensor(tmp[:, c, :], v[:, c, :], wide(stat[:, 1, c]), ALU.subtract))
                link(dve.tensor_tensor(agg[:, c, 0:D], tmp[:, c, :], tmp[:, c, :], ALU.mult))
                link(dve.tensor_reduce(stat[:, 2, c], agg[:, c, 0:D], AX_X, ALU.add))

            def normalise_relu():
                q = inverse_root(1.0 / D, 1e-5)
                for c in pieces:
                    link(dve.tensor_tensor(tmp[:, c, :], tmp[:, c, :], wide(q[:, c]), ALU.mult))
                    dve.tensor_scalar(h[:, c, :], tmp[:, c, :], 0.0, None, ALU.max).then_inc(s_h, 1)

            link(dve.memset(ones_row, 1.0))

            def buckets(key, blk, loc):
                as_int = mask.bitcast(I32)
                link(dve.tensor_scalar(as_int, key, -(BP // 2), 1.0 / BP, ALU.add, ALU.mult))
                link(dve.tensor_copy(blk, as_int))
                link(dve.scalar_tensor_tensor(out=loc, in0=blk, scalar=-float(BP), in1=key, op0=ALU.mult, op1=ALU.add))
                link(dve.scalar_tensor_tensor(out=blk, in0=loc, scalar=float(BP), in1=blk, op0=ALU.is_ge, op1=ALU.add))
                link(dve.tensor_scalar(mask, loc, 0.0, None, ALU.is_lt))
                link(dve.tensor_tensor(blk, blk, mask, ALU.subtract))
                link(dve.scalar_tensor_tensor(out=loc, in0=blk, scalar=-float(BP), in1=key, op0=ALU.mult, op1=ALU.add))

            def offsets(n):
                dve.wait_ge(s_pre, n + 1)
                link(dve.tensor_scalar(need_i[:, :], psum[0:EP, 0, 32:32 + NB], 127.0, None, ALU.add))
                link(dve.tensor_scalar(need_i[:, :], need_i[:, :], 7, None, ALU.logical_shift_right))
                link(dve.tensor_copy(need[:, :], need_i[:, :]))
                link(dve.tensor_tensor_scan(ends[:, n, :], ones_row[:, 0:NB], need[:, :], 0.0, ALU.mult, ALU.add))
                link(dve.tensor_tensor(base[:, n, :], ends[:, n, :], need[:, :], ALU.subtract))
                link(dve.tensor_scalar(base[:, n, :], base[:, n, :], 128.0, -1.0, ALU.mult, ALU.add))
                link(dve.tensor_tensor(base[:, n, :], base[:, n, :], psum[0:EP, 0, 0:NB], ALU.add))

            def place_bucket(n, b, is_b, link):
                half = EC // 2
                link(dve.tensor_tensor_scan(psum[0:EP, 1, 0:half], ones_row[:, 0:half], is_b[:, 0:half],
                                            base[:, n, b:b + 1], ALU.mult, ALU.add))
                link(dve.tensor_tensor_scan(psum[0:EP, 2, 0:half], ones_row[:, 0:half], is_b[:, half:EC],
                                            psum[0:EP, 1, half - 1:half], ALU.mult, ALU.add))
                link(dve.copy_predicated(pos.rearrange("p (a c) -> p a c", a=2),
                                         is_b.bitcast(I32).rearrange("p (a c) -> p a c", a=2),
                                         psum[0:EP, 1:3, 0:half]))

            def places_to_rows(row_out, link):
                row_i, tile_i = csum.bitcast(I32), prod.bitcast(I32)
                link(dve.tensor_copy(row_i, pos))
                link(dve.tensor_scalar(tile_i, row_i, 7, None, ALU.logical_shift_right))
                link(dve.tensor_scalar(row_i, row_i, 127, None, ALU.bitwise_and))
                link(dve.tensor_copy(mask, row_i))
                link(dve.tensor_copy(pos, tile_i))
                link(dve.scalar_tensor_tensor(out=row_out, in0=mask, scalar=float(T), in1=pos,
                                              op0=ALU.mult, op1=ALU.add))

            def from_banks(b):
                return psum[0:1, b:b + 2, 0:HALF_T]

            def in_halves(v):
                return v.rearrange("p (a t) -> p a t", a=2)

            def tiles_behind(n, step):
                dve.sem_inc(s_tg, 1)
                dve.wait_ge(s_tp, step + 1)
                link(dve.tensor_copy(bucket_col[:, 0:2 - n], psum[0:NB, 3, 0:2 - n]))
                link(dve.tensor_scalar(behind, iota_t[0:NB, :], bucket_col[:, 0:1], None, ALU.is_ge))
                dve.sem_inc(s_tg, 1)
                dve.wait_ge(s_tp, step + 2)

            def count_buckets(n, blk):
                for b in range(DVE_COUNTS[n]):
                    link(dve.tensor_scalar(mask, blk, float(b), None, ALU.is_equal, ALU.add,
                                           accum_out=count[:, n, b:b + 1]))

            dve.wait_ge(s_key, 4 * SPREAD + 32)
            link(dve.tensor_copy(meta[:, :, 1], key_d.bitcast(I32)))
            link(dve.tensor_copy(key_d, meta[:, :, 1]))
            link(dve.tensor_copy(mask, pos.bitcast(I32)))
            link(dve.tensor_tensor(mask, key_d, mask, ALU.is_gt))
            link(dve.tensor_reduce(count[:, 0, NB:NB + 1], mask, AX_X, ALU.max))
            buckets(key_d, blk_d, place)
            dve.sem_inc(s_blk, 1)
            count_buckets(0, blk_d)
            dve.sem_inc(s_cnt, 1)
            link(dve.tensor_copy(meta[:, :, 2], prod))
            link(dve.tensor_copy(meta[:, :, 0], csum.bitcast(I32)))
            buckets(meta[:, :, 0], blk_s, meta[:, :, 4])
            dve.sem_inc(s_blk, 1)
            offsets(0)
            dve.tensor_copy(unsorted[:, :], psum[0:1, 0, 32 + NB:33 + NB]).then_inc(s_flag, 1)
            dve.wait_ge(s_flag, 1)
            link(dve.scalar_tensor_tensor(out=waste[:, :], in0=need[:, :], scalar=128.0, in1=psum[0:EP, 0, 32:32 + NB],
                                          op0=ALU.mult, op1=ALU.subtract))
            count_buckets(1, blk_s)
            dve.sem_inc(s_cnt, 1)

            tiles_behind(0, 0)
            link(dve.tensor_copy(in_halves(blk_t[:, :]), psum[:, 3:5, 0:HALF_T]))
            link(dve.tensor_copy(in_halves(acc_d[:, :]), from_banks(5)))
            link(dve.tensor_scalar(sup_d[:, :], blk_t[0:1, :], float(D), None, ALU.mult))
            link(dve.tensor_scalar(start_row, iota_t[0:1, :], 128.0, None, ALU.mult))
            link(dve.tensor_tensor(in_halves(start_row), in_halves(start_row), from_banks(1), ALU.subtract))
            link(dve.tensor_scalar(start_row, start_row, float(E), None, ALU.min))
            link(dve.tensor_copy(start_d[:, :], start_row))
            offsets(1)
            tiles_behind(1, 2)
            link(dve.tensor_copy(in_halves(acc_s[:, :]), from_banks(5)))

            dve.wait_ge(s_x, SPREAD)
            centre(x, every)
            normalise_relu()

            general = [0]

            def general_link(ins):
                general[0] += 1
                ins.then_inc(s_gl, 1)
                dve.wait_ge(s_gl, general[0])

            with dve.If(dst_order(dve) > 0):
                for b in range(NB):
                    general_link(dve.tensor_scalar(mask, blk_d, float(b), None, ALU.is_equal))
                    place_bucket(0, b, mask, general_link)
                places_to_rows(place, general_link)
            for b in range(NB):
                dve.wait_ge(s_mask, b + 1)
                place_bucket(1, b, two_masks[:, b % 2, :], link)
                dve.sem_inc(s_mfre, 1)
            places_to_rows(meta[:, :, 3], link)
            dve.sem_inc(s_meta, 1)

            dve.wait_ge(s_rows, 1)
            dve.memset(sT[D:D + 1, :], 1.0).then_inc(s_norm, 1)

            def recall(k, i):
                dve.tensor_copy(node_d[:, k, :], node_all[:, bass.ds(i * BODY + k * GT, GT)]).then_inc(s_loc, 1)

            def one_hot(k, i, loop, node, weight=None):
                dve.wait_ge(s_used[k], i + (1 + loop * NI))
                for j in range(GT):
                    if weight is None:
                        ins = dve.tensor_scalar(hot[:, k, j, :], iota[:, 0:BP], node(j), None, ALU.is_equal)
                    else:
                        ins = dve.tensor_scalar(hot[:, k, j, :], iota[:, 0:BP], node(j), weight(j),
                                                ALU.is_equal, ALU.mult)
                ins.then_inc(s_hot[k], 1)

            def dst_hot(k, i, loop, weight=None):
                dve.wait_ge(s_loc, i * SETS + (k + 1 + loop * NI * SETS))
                one_hot(k, i, loop, lambda j: node_d[:, k, j:j + 1], weight)

            def locate_group(i, k):
                at = bass.ds(i * BODY + k * GT, GT)
                dve.wait_ge(s_used[k], i + 1)
                dve.wait_ge(s_ed[k], (i + 1) * (16 * GT))
                dve.scalar_tensor_tensor(out=node_d[:, k, :], in0=blk_t[:, at], scalar=-float(BP),
                                         in1=edges[:, k, :, 1], op0=ALU.mult, op1=ALU.add).then_inc(s_loc, 1)
                dve.tensor_copy(index[:, k, :], edges[:, k, :, 0]).then_inc(s_ix[k], 1)
                dst_hot(k, i, 0)
                dve.tensor_copy(index_all[:, at], edges[:, k, :, 0]).then_inc(s_keep, 1)
                dve.tensor_copy(node_all[:, at], node_d[:, k, :]).then_inc(s_keep, 1)

            def sum_group(i, k):
                dve.wait_ge(s_used[k], i + (1 + NI))
                recall(k, i)
                dve.tensor_copy(index[:, k, :], index_all[:, bass.ds(i * BODY + k * GT, GT)]).then_inc(s_ix[k], 1)
                dst_hot(k, i, 1)

            def tile_prepare(i, k):
                locate_group(i, k)
                dve.wait_ge(s_hot[k], i + 1)
                dve.tensor_scalar(pen[:, k, :, :], hot[:, k, :, :], BIG, -BIG, ALU.mult, ALU.add).then_inc(s_pen[k], 1)

            def tile_step(i, k, last):
                if not last:
                    tile_prepare(*following(i, k))
                dve.wait_ge(s_vt[k], i + 1)
                dve.wait_ge(s_exp[k], 2 * i + 1)
                dve.tensor_reduce(nmx[:, k, :], psum[0:BP, 5 + k % 2, :].rearrange("p (j e) -> p j e", j=GT),
                                  AX_X, ALU.max, negate=True).then_inc(s_mx[k], 1)
                dve.wait_ge(s_mx[k], i + 1)
                at = i * BODY + k * GT
                dve.tensor_copy(nmx_all[:, bass.ds(at, GT)], nmx[:, k, :]).then_inc(s_vl, 1)

            pipelined(dve, tile_prepare, tile_step)
            links[0] += NI * SETS
            dve.wait_ge(s_vl, links[0])

            def piece_evacuated(step, n):
                dve.wait_ge(s_ev, FIRST[step] + n + 1)

            for n, c in enumerate(pieces):
                piece_evacuated("z0", n)
                centre(z, c)
            q = inverse_root(1.0 / (D - 1), 0.0)
            for c in pieces:
                dve.tensor_tensor(h[:, c, :], z[:, c, :], wide(q[:, c]), ALU.mult).then_inc(s_h, 1)

            for k in range(SETS):
                dve.wait_ge(s_exp[k], 2 * NI + 1)
            link(dve.memset(nmx_full, 0.0))
            dve.wait_ge(s_keep, 2 * NI * SETS)

            def seg(ins, done):
                ins.then_inc(s_sg, 1)
                dve.wait_ge(s_sg, done)

            with dve.Fori(0, NB) as i:
                is_b = iota[0:BP, bass.ds(i, 1)]
                seg_m_b = seg_m[:, bass.ds(i, 1)]
                sum_group(i, 0)
                seg(dve.tensor_scalar(seg_tmp, blk_t[0:BP, :], is_b, BIG, ALU.not_equal, ALU.mult), i * 5 + 1)
                seg(dve.tensor_tensor(seg_tmp, seg_tmp, nmx_all, ALU.add), i * 5 + 2)
                sum_group(i, 1)
                seg(dve.tensor_reduce(seg_m_b, seg_tmp, AX_X, ALU.min), i * 5 + 3)
                sum_group(i, 2)
                seg(dve.tensor_scalar(seg_tmp, blk_t[0:BP, :], is_b, seg_m_b, ALU.is_equal, ALU.mult), i * 5 + 4)
                sum_group(i, 3)
                seg(dve.tensor_tensor(nmx_full, nmx_full, seg_tmp, ALU.add), i * 5 + 5)
            dve.tensor_tensor(nmx_full, nmx_full, nmx_all, ALU.subtract).then_inc(s_seg, 1)
            for k in range(SETS):
                sum_group(NB, k)
            dve.wait_ge(s_segx, 1)
            seg(dve.tensor_tensor(den_all, den_all, nmx_full, ALU.mult), 5 * NB + 1)
            with dve.Fori(NB + 1, NI) as i:
                b = i - (NB + 1)
                sum_group(i, 0)
                seg(dve.tensor_scalar(seg_tmp, blk_t[0:BP, :], iota[0:BP, bass.ds(b, 1)], None, ALU.is_equal),
                    b * 3 + (5 * NB + 2))
                sum_group(i, 1)
                seg(dve.tensor_tensor(seg_tmp, seg_tmp, den_all, ALU.mult), b * 3 + (5 * NB + 3))
                sum_group(i, 2)
                seg(dve.tensor_reduce(seg_d[:, bass.ds(b, 1)], seg_tmp, AX_X, ALU.add), b * 3 + (5 * NB + 4))
                sum_group(i, 3)
            link(dve.tensor_scalar(seg_m[:, :], seg_m[:, :], BIG / 2, None, ALU.is_lt))
            link(dve.tensor_tensor(seg_d[:, :], seg_d[:, :], seg_m[:, :], ALU.mult))
            link(dve.tensor_scalar(share[:, :], seg_d[:, :], 1e-30, None, ALU.max))
            link(dve.reciprocal(seg_m[:, :], share[:, :]))
            link(dve.tensor_tensor(share[:, :], seg_d[:, :], seg_m[:, :], ALU.mult))
            for n, c in enumerate(pieces):
                piece_evacuated("z1", n)
                centre(z, c)
            q = inverse_root(1.0 / (D - 1), 0.0)
            link(dve.tensor_tensor(z[:, :, :], z[:, :, :], wide(q), ALU.mult))
            link(dve.tensor_tensor(x[:, :, :], x[:, :, :], z[:, :, :], ALU.add))
            centre(x, every)
            normalise_relu()

            for n, c in enumerate(pieces):
                piece_evacuated("y", n)
                link(dve.tensor_tensor(z[:, c, :], z[:, c, :], wide(share[:, c]), ALU.mult))
                link(dve.tensor_tensor(x[:, c, :], x[:, c, :], z[:, c, :], ALU.add))
                centre(x, c)
            normalise_relu()

            def message_step(i, k, last):
                if ahead(i, k, 2):
                    message_hot(*ahead(i, k, 2))
                dve.wait_ge(s_mfree[k], i + 1)
                dve.wait_ge(s_row, i * (2 * SETS) + (2 * k + 2))
                dve.tensor_copy(index[:, k, :], row_s[:, k, :]).then_inc(s_ix[k], 1)
                dve.tensor_copy(msg[:, k, :, D], edges[:, k, :, 4]).then_inc(s_edf[k], 1)
                dve.wait_ge(s_sup[k], i + 1)
                dve.tensor_copy(msg[:, k, :, 0:D],
                                psum[:, k, 0:GT * D].rearrange("p (j f) -> p j f", j=GT)).then_inc(s_msg[k], 1)

            def message_hot(i, k):
                dve.wait_ge(s_ed[k], (i + (1 + NI)) * (16 * GT))
                recall(k, i)
                dst_hot(k, i, 2, lambda j: edges[:, k, j, 2:3])
                dve.tensor_scalar(row_s[:, k, :], node_d[:, k, :], BP - 0.5, float(ROWS), ALU.is_ge,
                                  ALU.mult).then_inc(s_row, 1)
                dve.wait_ge(s_row, i * (2 * SETS) + (2 * k + 1))
                dve.tensor_tensor(row_s[:, k, :], row_s[:, k, :], edges[:, k, :, 3], ALU.add).then_inc(s_row, 1)

            def message_first(i, k):
                message_hot(0, 0)
                message_hot(0, 1)

            pipelined(dve, message_first, message_step)

            link(dve.tensor_tensor(x[:, :, :], x[:, :, :], l2b[:, :].unsqueeze(1).broadcast_to([BP, NB, D]), ALU.add))
            with dve.Fori(0, NI) as i:
                for k in range(SETS):
                    dve.wait_ge(s_ml[k], (i + 1) * 16)
                    one_hot(k, i, 3, lambda j: msg[:, k, j, D:D + 1])
            for n, c in enumerate(pieces):
                dve.wait_ge(s_agg, 2 * len(pieces) + n + 1)
                link(dve.tensor_tensor(x[:, c, :], x[:, c, :], agg[:, c, 0:D], ALU.add))
                centre(x, c)
            normalise_relu()
            link(dve.tensor_tensor(x[:, :, :], x[:, :, :], ln_b[:, :].unsqueeze(1).broadcast_to([BP, NB, D]), ALU.add))

            link(dve.tensor_scalar(gw2[:, :], gw2[:, :], 0.5, None, ALU.mult))
            link(dve.tensor_scalar(gb2[:, :], gb2[:, :], 0.5, None, ALU.mult))
            for k in range(SETS):
                dve.wait_ge(s_used[k], 1 + 4 * NI)
            link(dve.memset(gel[:, :, :, 0, D:D + 1].rearrange("p k j n -> p (k j) n"), 1.0))
            def split(parts, value, rest, step):
                step(dve.tensor_copy(parts(0), value))
                step(dve.tensor_tensor(rest, value, parts(0), ALU.subtract))
                step(dve.tensor_copy(parts(1), rest))
                return dve.tensor_tensor(parts(2), rest, parts(1), ALU.subtract)

            def edge_index(i, k):
                dve.wait_ge(s_hid[k], i * 2 + 2)
                dve.tensor_copy(index[:, k, :], index_all[:, bass.ds(i * BODY + k * GT, GT)]).then_inc(s_ix[k], 1)

            def edge_prepare(i, k):
                recall(k, i)
                dve.wait_ge(s_fe[k], (i + 1) * (16 * GT))
                done = [0]

                def step(ins):
                    done[0] += 1
                    ins.then_inc(s_sp, 1)
                    dve.wait_ge(s_sp, (i * SETS + k) * 4 + done[0])

                step(split(lambda m: attr_parts[:, k, :, m, :], edges[:, k, :, 5:PW], attr_rest[:, k, :, :], step))
                dve.sem_inc(s_atp[k], 1)
                dve.sem_inc(s_edf[k], 1)

            def edge_step(i, k, last):
                dve.wait_ge(s_gel[k], i * 2 + 2)
                if ahead(i, k, SETS):
                    edge_index(*ahead(i, k, SETS))
                dve.tensor_tensor(gprod[:, :, :], gel[:, k, :, 1, 0:D],
                                  gw2[:, :].unsqueeze(1).broadcast_to([128, GT, D]), ALU.mult).then_inc(s_prod, 1)
                dve.wait_ge(s_prod, i * SETS + (k + 1))
                dve.tensor_reduce(gsum[:, k, :], gprod[:, :, :], AX_X, ALU.add).then_inc(s_dot[k], 1)
                if ahead(i, k, 3):
                    edge_prepare(*ahead(i, k, 3))
                dve.wait_ge(s_gate, i * SETS + (k + 1))
                dve.tensor_scalar(gate[:, k, :], gsum[:, k, :], 0.5, 0.5, ALU.mult, ALU.add).then_inc(s_gst, 1)
                dve.wait_ge(s_gst, i * SETS + (k + 1))
                dve.wait_ge(s_loc, i * SETS + (k + 1 + 3 * NI * SETS))
                one_hot(k, i, 4, lambda j: node_d[:, k, j:j + 1], lambda j: gate[:, k, j:j + 1])

            tab3 = tab[:, :].rearrange("p (b f) -> p b f", f=2 * D)
            for c in pieces:
                dve.wait_ge(s_ev, FIRST["tab3"] + -(-c.stop // 2))
                split(lambda m: tab_parts[:, c, m, :], tab3[:, c, :], tab3[:, c, :], link).then_inc(s_parts, 1)
            link(dve.tensor_copy(ident_b[:, :], ident[:, :]))
            we = wt[0:3 * DE, WI["mW1e"]:WI["mW1e"] + 2, :].rearrange("p w f -> p (w f)")
            link(split(lambda m: we_parts[:, m, :], we, we, link))
            dve.wait_ge(s_tab, SPREAD * (2 + len(pieces)))
            dve.sem_inc(s_norm, 1)

            def edge_first(i, k):
                for n in range(SETS):
                    edge_index(0, n)
                for n in range(3):
                    edge_prepare(0, n)

            pipelined(dve, edge_first, edge_step)

            dve.wait_ge(s_mm, FIRST["msgT"] + SIZE["msgT"])
            dve.memset(aT[D:D + 1, :], 1.0).then_inc(s_norm, 1)
            for n, c in enumerate(pieces):
                piece_evacuated("up", n)
                link(dve.tensor_tensor(z[:, c, :], z[:, c, :], h[:, c, :], ALU.add))
                centre(z, c)
            q = inverse_root(1.0 / D, 1e-5)
            for c in pieces:
                link(dve.tensor_tensor(tmp[:, c, :], tmp[:, c, :], wide(q[:, c]), ALU.mult))
                link(dve.tensor_tensor(tmp[:, c, :], tmp[:, c, :],
                                       ln_g[:, :].unsqueeze(1).broadcast_to([BP, PER_BANK, D]), ALU.mult))
                dve.tensor_tensor(z[:, c, :], x[:, c, :], tmp[:, c, :], ALU.add).then_inc(s_res, 1)

        @block.scalar
        def _(act):
            roots = [0]

            def root():
                act.wait_ge(s_var, roots[0] + 1)
                act.activation(stat[:, 3, :], stat[:, 2, :], ACT.Sqrt).then_inc(s_sd, 1)
                roots[0] += 1

            def evacuate(step, dst, src, func=ACT.Copy):
                for j in range(SIZE[step]):
                    g = FIRST[step] + j
                    act.wait_ge(s_mm, g + 1)
                    act.activation(dst(j), src(j, psum[:, node_bank(g), :]), func).then_inc(s_ev, 1)

            def turned(to, rows=D):
                return (lambda j: to[0:rows, 4 * BP * j:min(4 * BP * (j + 1), N)],
                        lambda j, bank: bank[0:rows, 0:min(4 * BP, N - 4 * BP * j)])

            def blocks(to):
                return (lambda j: to[:, 5 * j:5 * j + 5, :].rearrange("p b f -> p (b f)"),
                        lambda j, bank: bank[0:BP, 0:5 * D])

            tab_b = tab[:, 0:NB * D].rearrange("p (b f) -> p b f", f=D)

            def aggregate(loop, n):
                for k in range(SETS):
                    act.wait_ge(s_used[k], 1 + (loop + 1) * NI)
                for j in range(5):
                    act.activation(agg[:, 5 * j:5 * j + 5, :].rearrange("p b f -> p (b f)"),
                                   psum[0:BP, j, 0:5 * AW], ACT.Copy).then_inc(s_agg, 1)

            def count_buckets(n, blk, first):
                for b in range(first, NB):
                    m = links[0] % 2
                    links[0] += 1
                    act.activation(two_masks[:, m, :], blk, ACT.Abs, bias=minus_b[:, b:b + 1]).then_inc(s_al, 1)
                    act.wait_ge(s_al, 2 * links[0] - 1)
                    act.activation(two_masks[:, m, :], two_masks[:, m, :], ACT.Relu, bias=ones[0:EP, 0:1], scale=-1.0,
                                   accum_out=count[:, n, b:b + 1]).then_inc(s_al, 1)
                    act.wait_ge(s_al, 2 * links[0])
                act.sem_inc(s_cact, 1)

            links = [0]
            act.wait_ge(s_blk, 1)
            count_buckets(0, blk_d, DVE_COUNTS[0])
            act.wait_ge(s_blk, 2)
            count_buckets(1, blk_s, DVE_COUNTS[1])

            root()
            evacuate("h0T", *turned(hT))
            evacuate("tab0", *blocks(tab_b))

            act.wait_ge(s_meta, 1)
            with act.If(dst_order(act) > 0):
                with act.Fori(0, NIS) as i:
                    for k in range(SETS):
                        act.wait_ge(s_fr[k], i + 1)
                        act.activation(place_slot[:, k, :], place[:, bass.ds(i * BODY + k * GT, GT)], ACT.Copy)
                        act.activation(edges[0:EP, k, :, 0:META], meta[:, bass.ds(i * BODY + k * GT, GT), :],
                                       ACT.Copy).then_inc(s_ms[k], 1)

            act.wait_ge(s_rows, 1)
            evacuate("self0", *turned(sT))

            act.wait_ge(s_padm, 16 * NI)
            for k in range(SETS):
                act.sem_inc(s_exp[k], 1)
            def masked_weights(i, k):
                act.wait_ge(s_pen[k], i + 1)
                for j in range(GT):
                    ins = act.activation(val[:, k, j, :], pen[:, k, j, :], ACT.Identity, bias=edges[:, k, j, 2:3])
                ins.then_inc(s_val[k], 1)

            def tile_step(i, k, last):
                if not last:
                    masked_weights(*following(i, k))
                act.wait_ge(s_mx[k], i + 1)
                for j in range(GT):
                    at = psum[0:BP, 5 + k % 2, 128 * j:128 * j + 128]
                    ins = act.activation(at, at, ACT.Exp, bias=nmx[:, k, j:j + 1], accum_out=den[:, k, j:j + 1])
                ins.then_inc(s_exp[k], 1)
                act.wait_ge(s_exp[k], 2 * i + 2)
                act.activation(den_all[:, bass.ds(i * BODY + k * GT, GT)], den[:, k, :], ACT.Copy).then_inc(s_exp[k], 1)

            pipelined(act, masked_weights, tile_step)

            aggregate(0, 1)
            evacuate("agg0T", *turned(aT))
            evacuate("z0", *blocks(z))
            root()
            evacuate("h1T", *turned(hT))
            act.wait_ge(s_tab, SPREAD)
            evacuate("tab1", *blocks(tab_b))
            evacuate("self1", *turned(sT))
            with act.Fori(0, NB) as i:
                act.wait_ge(s_used[0], i + (2 + NI))
                piece = bass.ds(i * (E // NB), E // NB)
                act.dma_start(attr_sorted[piece, :].rearrange("(p c) f -> p (c f)", p=80),
                              a["edge_attr_32"][piece, :].rearrange("(p c) f -> p (c f)", p=80)).then_inc(s_copy, 16)
            act.wait_ge(s_seg, 1)
            act.activation(nmx_full, nmx_full, ACT.Exp).then_inc(s_segx, 1)
            aggregate(1, 2)
            evacuate("agg1T", *turned(aT))
            evacuate("z1", *blocks(z))
            root()
            root()
            evacuate("h2T", *turned(hT))
            evacuate("y", *blocks(z), func=ACT.Relu)
            root()
            evacuate("h3T", *turned(hT))
            act.wait_ge(s_tab, 2 * SPREAD)
            evacuate("sup", *blocks(tab_b))

            def turned_hot(i, k):
                act.wait_ge(s_used[k], i + (2 + 2 * NI))
                act.activation(hotT[:, k, :], psum[0:BP, 5 + k % 2, :], ACT.Copy).then_inc(s_hte[k], 1)

            for k in range(SETS):
                turned_hot(0, k)
                act.sem_inc(s_mfree[k], 1)
            with act.Fori(1, NI) as i:
                for k in range(SETS):
                    turned_hot(i, k)
                    act.wait_ge(s_msc[k], i * (16 * GT))
                    act.sem_inc(s_mfree[k], 1)

            aggregate(3, 3)
            root()
            evacuate("h4T", *turned(hT))
            evacuate("tab3",
                     lambda j: tab[:, 4 * D * j:min(4 * D * (j + 1), 2 * D * NB)],
                     lambda j, bank: bank[0:BP, 0:min(4 * D, 2 * D * (NB - 2 * j))])

            def turn_attr(i, k):
                act.wait_ge(s_attT[k], i + 1)
                act.activation(attrT[:, k, :], attr_bank, ACT.Copy).then_inc(s_atte[k], 1)

            def hidden(i, k):
                for half in range(2):
                    act.wait_ge(s_hid[k], i * 2 + (3 + half))
                    act.activation(gel[:, k, 2 * half:2 * half + 2, :, 0:D],
                                         psum[:, 6 + half, 0:4 * D].rearrange("p (j s f) -> p j s f", j=2, s=2),
                                   ACT.Gelu).then_inc(s_gel[k], 1)

            def edge_step(i, k, last):
                act.wait_ge(s_dot[k], i + 1)
                act.activation(gsum[:, k, :], gsum[:, k, :], ACT.Tanh, bias=gb2[:, 0:1]).then_inc(s_gate, 1)
                if ahead(i, k, 2):
                    turn_attr(*ahead(i, k, 2))
                if ahead(i, k, 1):
                    hidden(*ahead(i, k, 1))

            def edge_first(i, k):
                turn_attr(0, 0)
                hidden(0, 0)
                turn_attr(0, 1)

            pipelined(act, edge_first, edge_step)

            aggregate(4, 4)
            evacuate("agg3T", *turned(aT, D + 1))
            evacuate("msgT", *turned(sT))
            act.wait_ge(s_norm, 3)
            evacuate("uT", *turned(aT), func=ACT.Gelu)
            evacuate("up", *blocks(z))
            root()

        @block.tensor
        def _(pe):
            def open_group(g):
                if g >= 3:
                    pe.wait_ge(s_ev, g - 2)
                return psum[:, node_bank(g), :]

            def chunk(j):
                return 4 * BP * j, min(4 * BP, N - 4 * BP * j)

            def transpose_blocks(step, src, ready, nth, rows=D):
                for j in range(SIZE[step]):
                    bank = open_group(FIRST[step] + j)
                    pe.wait_ge(ready, nth * (NB // PER_BANK) + pieces_for(j))
                    for q in range(min(4, NB - 4 * j)):
                        ins = pe.transpose(bank[0:rows, BP * q:BP * q + BP], src[:, 4 * j + q, 0:rows], ident[0:BP, 0:BP])
                    ins.then_inc(s_mm, 1)

            def to_nodes(step, terms):
                for j in range(SIZE[step]):
                    bank = open_group(FIRST[step] + j)
                    for q in range(5):
                        b = 5 * j + q
                        for m, (lhs, rows, w) in enumerate(terms):
                            ins = pe.matmul(bank[0:BP, D * q:D * q + D], lhs[0:rows, BP * b:BP * b + BP],
                                            wt[0:rows, WI[w], :], start=(m == 0), stop=(m == len(terms) - 1))
                    ins.then_inc(s_mm, 1)

            def to_features(step, terms):
                for j in range(SIZE[step]):
                    bank = open_group(FIRST[step] + j)
                    lo, n = chunk(j)
                    for m, (rhs, rows, w) in enumerate(terms):
                        ins = pe.matmul(bank[0:D, 0:n], wt[0:rows, WI[w], :], rhs[0:rows, lo:lo + n],
                                        start=(m == 0), stop=(m == len(terms) - 1))
                    ins.then_inc(s_mm, 1)

            def evacuated(step):
                pe.wait_ge(s_ev, FIRST[step] + SIZE[step])

            def zero_sums():
                for j in range(5):
                    pe.matmul(psum[0:BP, j, :], zrow[:, 0:BP], zrow[:, :], start=True, stop=True)

            def add_tile(k, j, cols, rhs):
                width = rhs.shape[-1]
                return pe.matmul(acc[:, bass.ds(cols[k * GT + j], width)], hot[:, k, j, :], rhs,
                                 start=False, stop=True, skip_group_check=True)

            def columns(tbl, top, i):
                return nc.values_load_multi_w_load_instructions(
                    tbl[0:1, bass.ds(i * BODY, BODY)], engines=(mybir.EngineType.PE,), min_val=0, max_val=top,
                    skip_runtime_bounds_check_because="the table holds the columns of blocks 0 to 24 only")[1]

            cols = [None] * BODY
            ACC_TOP = 4 * 512 + 4 * AW
            SUP_TOP = (NB - 1) * D

            pe.wait_ge(s_const, 1)

            def sum_counts(n):
                pe.wait_ge(s_cnt, n + 1)
                pe.wait_ge(s_cact, n + 1)
                wide = NB + 1 - n
                pe.matmul(psum[0:EP, 0, 0:NB], upper[0:EP, 0:EP], count[:, n, 0:NB], start=True, stop=True)
                pe.matmul(psum[0:EP, 0, 32:32 + wide], ones[0:EP, 0:EP], count[:, n, 0:wide],
                          start=True, stop=True).then_inc(s_pre, 1)

            def turn_row(to, v):
                return pe.matmul(to, v, ones[0:1, 0:1], start=True, stop=True)

            def tile_table(b, weights, n_buckets):
                for half in range(2):
                    ins = pe.matmul(psum[0:weights.shape[-1], b + half, 0:HALF_T], weights,
                                    behind[0:n_buckets, HALF_T * half:HALF_T * half + HALF_T], start=True, stop=True)
                return ins

            sum_counts(0)
            pe.wait_ge(s_tg, 1)
            turn_row(psum[0:NB, 3, 0:1], ends[0:1, 0, :])
            turn_row(psum[0:NB, 3, 1:2], waste[0:1, :]).then_inc(s_tp, 1)
            pe.wait_ge(s_tg, 2)
            tile_table(3, ones[0:NB - 1, :], NB - 1)
            tile_table(5, bucket_col[0:NB - 1, 2:3], NB - 1)
            tile_table(1, bucket_col[:, 1:2], NB).then_inc(s_tp, 1)
            sum_counts(1)
            pe.wait_ge(s_tg, 3)
            turn_row(psum[0:NB, 3, 0:1], ends[0:1, 1, :]).then_inc(s_tp, 1)
            pe.wait_ge(s_tg, 4)
            tile_table(5, bucket_col[0:NB - 1, 2:3], NB - 1).then_inc(s_tp, 1)
            pe.wait_ge(s_w, 16 * WEIGHT_LOADS)
            transpose_blocks("h0T", h, s_h, 0)
            evacuated("h0T")
            to_nodes("tab0", [(hT, D + 1, "W0_0")])

            to_features("self0", [(hT, D + 1, "W1_0")])

            for k in range(SETS):
                pe.sem_inc(s_used[k], 1)
            evacuated("self0")
            zero_sums()
            def turn_weights(i, k):
                pe.wait_ge(s_val[k], i + 1)
                pe.wait_ge(s_exp[(k + 2) % 4], 2 * i + (1 if k < 2 else 2))
                for j in range(GT):
                    ins = pe.transpose(psum[0:BP, 5 + k % 2, 128 * j:128 * j + 128], val[:, k, j, :], ident[:, :])
                ins.then_inc(s_vt[k], 1)

            def tile_step(i, k, last):
                if not last:
                    turn_weights(*following(i, k))
                if k == 0:
                    cols[:] = columns(acc_d, ACC_TOP, i)
                pe.wait_ge(s_hot[k], i + 1)
                pe.wait_ge(s_g[k], (i + 1) * (16 * GT))
                for j in range(GT):
                    ins = add_tile(k, j, cols, gat[:, k, j, 0:D])
                ins.then_inc(s_used[k], 1)

            pipelined(pe, turn_weights, tile_step)
            for k in range(SETS):
                pe.wait_ge(s_exp[k], 2 * NI + 1)
            transpose_blocks("agg0T", agg, s_agg, 0)
            evacuated("agg0T")
            pe.wait_ge(s_norm, 1)
            to_nodes("z0", [(sT, D + 1, "W2a_0"), (aT, D, "W2b_0")])
            transpose_blocks("h1T", h, s_h, 1)
            evacuated("h1T")
            to_nodes("tab1", [(hT, D + 1, "W0_1")])
            to_features("self1", [(hT, D + 1, "W1_1")])

            evacuated("self1")
            zero_sums()
            with pe.Fori(0, NI) as i:
                cols[:] = columns(acc_d, ACC_TOP, i)
                for k in range(SETS):
                    pe.wait_ge(s_hot[k], i + (1 + NI))
                    pe.wait_ge(s_g[k], (i + (1 + NI)) * (16 * GT))
                    for j in range(GT):
                        ins = add_tile(k, j, cols, gat[:, k, j, 0:D])
                    ins.then_inc(s_used[k], 1)
            transpose_blocks("agg1T", agg, s_agg, 1)
            evacuated("agg1T")
            to_nodes("z1", [(sT, D + 1, "W2a_1"), (aT, D, "W2b_1")])

            transpose_blocks("h2T", h, s_h, 2)
            evacuated("h2T")
            to_nodes("y", [(hT, D + 1, "Wv")])

            transpose_blocks("h3T", h, s_h, 3)
            evacuated("h3T")
            to_nodes("sup", [(hT, D, "Wl2")])
            evacuated("sup")
            def turn_hot(i, k):
                pe.wait_ge(s_hot[k], i + (1 + 2 * NI))
                for j in range(GT):
                    ins = pe.transpose(psum[0:BP, 5 + k % 2, 128 * j:128 * j + 128], hot[:, k, j, :], ident[:, :])
                ins.then_inc(s_used[k], 1)

            def message_step(i, k, last):
                if not last:
                    turn_hot(*following(i, k))
                if k == 0:
                    cols[:] = columns(sup_d, SUP_TOP, i)
                pe.wait_ge(s_hte[k], i + 1)
                for j in range(GT):
                    ins = pe.matmul(psum[:, k, D * j:D * j + D], hotT[:, k, 128 * j:128 * j + 128],
                                    tab[:, bass.ds(cols[k * GT + j], D)], start=True, stop=True)
                ins.then_inc(s_sup[k], 1)

            pipelined(pe, turn_hot, message_step)
            for k in range(SETS):
                pe.wait_ge(s_msg[k], NI)
            zero_sums()
            with pe.Fori(0, NI) as i:
                cols[:] = columns(acc_s, ACC_TOP, i)
                for k in range(SETS):
                    pe.wait_ge(s_hot[k], i + (1 + 3 * NI))
                    pe.wait_ge(s_ml[k], (i + 1) * 16)
                    for j in range(GT):
                        ins = add_tile(k, j, cols, msg[:, k, j, 0:D])
                    ins.then_inc(s_used[k], 1)

            transpose_blocks("h4T", h, s_h, 4)
            evacuated("h4T")
            for j in range(SIZE["tab3"]):
                bank = open_group(FIRST["tab3"] + j)
                for q in range(min(2, NB - 2 * j)):
                    b = 2 * j + q
                    for half, w in enumerate(("mW1x", "gW1x")):
                        ins = pe.matmul(bank[0:BP, D * (2 * q + half):D * (2 * q + half) + D], hT[0:D + 1, BP * b:BP * b + BP],
                                        wt[0:D + 1, WI[w], :], start=True, stop=True)
                ins.then_inc(s_mm, 1)
            evacuated("tab3")
            zero_sums()
            def turn_attr(i, k):
                pe.wait_ge(s_atp[k], i + 1)
                for j in range(GT):
                    ins = pe.transpose(attr_bank[:, 128 * j:128 * j + 128],
                                       attr_parts[:, k, j, :, :].rearrange("p s f -> p (s f)"), ident_b[:, :])
                ins.then_inc(s_attT[k], 1)

            def edge_part(i, k, first=False):
                pe.wait_ge(s_atte[k], i + 1)
                pe.wait_ge(s_g[k], (i + (1 + 2 * NI)) * (16 * GT))
                for j in range(GT):
                    if j % 2 == 0:
                        if k:
                            pe.wait_ge(s_gel[k - 1], i * 2 + (1 + j // 2))
                        elif not first:
                            pe.wait_ge(s_gel[SETS - 1], i * 2 + (j // 2 - 1))
                    to = psum[:, 6 + j // 2, 2 * D * (j % 2):2 * D * (j % 2) + 2 * D]
                    for m in range(3):
                        pe.matmul(to, attrT[:, k, 128 * j:128 * j + 128], we_parts[:, m, :], start=(m == 0), stop=False)
                    for m in range(3):
                        ins = pe.matmul(to, ident_b[:, :], gat3[:, k, j, 2 * D * m:2 * D * m + 2 * D], start=False, stop=(m == 2))
                    if j % 2 == 1:
                        ins.then_inc(s_hid[k], 1)

            def edge_step(i, k, last):
                if ahead(i, k, 1):
                    edge_part(*ahead(i, k, 1))
                if ahead(i, k, 2):
                    turn_attr(*ahead(i, k, 2))
                if k == 0:
                    cols[:] = columns(acc_d, ACC_TOP, i)
                for g in {0: (), 1: (0,), 2: (1,), 3: (2, 3)}[k]:
                    pe.wait_ge(s_hot[g], i + (1 + 4 * NI))
                    for j in range(GT):
                        ins = add_tile(g, j, cols, gel[:, g, j, 0, :])
                    ins.then_inc(s_used[g], 1)

            def edge_first(i, k):
                turn_attr(0, 0)
                edge_part(0, 0, first=True)
                turn_attr(0, 1)

            pe.wait_ge(s_norm, 2)
            for k in range(SETS):
                pe.sem_inc(s_hid[k], 2)
            pipelined(pe, edge_first, edge_step)
            transpose_blocks("agg3T", agg, s_agg, 3, D + 1)
            evacuated("agg3T")
            to_features("msgT", [(aT, D + 1, "mW2")])
            evacuated("msgT")
            to_features("uT", [(hT, D + 1, "uW1a"), (sT, D, "uW1b")])
            evacuated("uT")
            to_nodes("up", [(aT, D + 1, "uW2")])


_INS = ["x", "src", "dst", "edge_attr_32", "edge_weight", "L0_gnn_W0", "L0_gnn_b0", "L0_gnn_W1", "L0_gnn_b1",
        "L0_gnn_W2", "L0_gnn_b2", "L1_gnn_Wv", "L1_gnn_bv", "L2_gnn_weight", "L2_gnn_b",
        "L3_gnn_mW1", "L3_gnn_mb1", "L3_gnn_mW2", "L3_gnn_mb2", "L3_gnn_gW1", "L3_gnn_gb1", "L3_gnn_gW2",
        "L3_gnn_gb2", "L3_gnn_uW1", "L3_gnn_ub1", "L3_gnn_uW2", "L3_gnn_ub2", "L3_gnn_ln_g", "L3_gnn_ln_b"]


def kernel(**inputs):
    import numpy as _np
    import concourse.bacc as _bacc
    from concourse import mybir as _mybir
    from concourse.bass_utils import run_bass_kernel_spmd as _run

    nc = _bacc.Bacc("TRN2", target_bir_lowering=False, num_devices=1)
    arrays, aps = {}, {}
    for name in _INS:
        v = _np.ascontiguousarray(inputs[name])
        arrays[f"in_{name}_dram"] = v
        aps[name] = nc.dram_tensor(f"in_{name}_dram", v.shape, _mybir.dt.from_np(v.dtype), kind="ExternalInput").ap()
    out = nc.dram_tensor("out_0_dram", (N, D), _mybir.dt.float32, kind="ExternalOutput").ap()
    build(nc, aps, out)
    r = _run(nc, [arrays], core_ids=[0])
    return r.results[0]["out_0_dram"]
```
